# Optimizing a Trainium2 kernel written in Bass

```python
import numpy as np
import jax
import jax.numpy as jnp

def _softmax(x, axis=-1):
    return jax.nn.softmax(x, axis=axis)

def _gelu(x):
    return jax.nn.gelu(x, approximate=True)

def _silu(x):
    return jax.nn.silu(x)

def _sigmoid(x):
    return jax.nn.sigmoid(x)

def _layernorm(x, axis=-1, eps=1e-05):
    m = jnp.mean(x, axis=axis, keepdims=True)
    v = jnp.var(x, axis=axis, keepdims=True)
    return (x - m) / jnp.sqrt(v + eps)

def _scatter_add(tgt, idx, src, axis=0):
    return tgt.at[idx].add(src)

def _segment_sum(src, seg, n):
    return jax.ops.segment_sum(src, seg, n)
kernel_name = 'mk_lm_tower_d1_tok_ids1024_r4_07c82b'

def setup_inputs(seed: int=0):
    np.random.seed(seed)
    _w = jnp.asarray

    def _rec_inputs():
        import jax
        import jax.numpy as jnp
        _rk = jax.random.key(seed)
        x = jax.random.randint(jax.random.fold_in(_rk, 1), (2, 1024), 0, 12564, jnp.int32)
        return x
    x = _rec_inputs()

    def _L0_tok_setup():
        import jax, jax.numpy as jnp
        import numpy as np
        VOCAB = 50257
        D_MODEL = 256
        BATCH = 4
        SEQ = 1024
        key = jax.random.key(seed)
        k_x, k_w = jax.random.split(key)
        x = jax.random.randint(k_x, (BATCH, SEQ), 0, VOCAB, dtype=jnp.int64 if jax.config.jax_enable_x64 else jnp.int32)
        W = jax.random.truncated_normal(k_w, -3.0, 3.0, (VOCAB, D_MODEL), dtype=jnp.float32)
        return {'x': x, 'W': W}
    _L0_tok_all = _L0_tok_setup()
    _L0_tok_in = {k: v for k, v in _L0_tok_all.items() if k in ('W',)}
    del _L0_tok_all

    def _L0_attn_setup():
        import jax, jax.numpy as jnp
        import numpy as np
        B, S, HID = (4, 256, 256)
        H, D = (16, 64)
        NEG_INF = -10000000000.0

        def rope_alternate(inputs, position, min_timescale=1.0, max_timescale=10000.0):
            d = inputs.shape[-1]
            half = d // 2
            fraction = 2.0 * jnp.arange(half, dtype=jnp.float32) / d
            timescale = min_timescale * (max_timescale / min_timescale) ** fraction
            sinusoid = position[:, :, None, None] / timescale
            sin, cos = (jnp.sin(sinusoid), jnp.cos(sinusoid))
            first, second = jnp.split(inputs, 2, axis=-1)
            return jnp.concatenate([(first * cos - second * sin).astype(inputs.dtype), (second * cos + first * sin).astype(inputs.dtype)], axis=-1)
        key = jax.random.key(seed)
        k1, k2, k3 = jax.random.split(key, 3)
        x = jax.random.normal(k1, (B, S, HID), dtype=jnp.float32)
        wqkv = jax.random.normal(k2, (HID, 3 * H * D), dtype=jnp.float32) * (1.0 / np.sqrt(HID))
        wo = jax.random.normal(k3, (H * D, HID), dtype=jnp.float32) * (1.0 / np.sqrt(H * D))
        return {'x': x, 'wqkv': wqkv, 'wo': wo}
    _L0_attn_all = _L0_attn_setup()
    _L0_attn_in = {k: v for k, v in _L0_attn_all.items() if k in ('wqkv', 'wo')}
    del _L0_attn_all

    def _L0_ffn_setup():
        import jax, jax.numpy as jnp
        import numpy as np
        H = 256
        I = 704
        E = 8
        TOP_K = 2

        def _moe(hidden_states, router_w, gate_w, up_w, down_w):
            B, S, Hd = hidden_states.shape
            x = hidden_states.reshape(-1, Hd)
            logits = x @ router_w.T
            probs = jax.nn.softmax(logits.astype(jnp.float32), axis=-1)
            top_w, top_idx = jax.lax.top_k(probs, TOP_K)
            top_w = top_w.astype(x.dtype)
            onehot = jax.nn.one_hot(top_idx, E, dtype=x.dtype)
            w_te = jnp.einsum('tk,tke->te', top_w, onehot)
            g = jnp.einsum('th,eih->tei', x, gate_w)
            u = jnp.einsum('th,eih->tei', x, up_w)
            h = jax.nn.silu(g) * u
            y = jnp.einsum('tei,ehi,te->th', h, down_w, w_te)
            return y.reshape(B, S, Hd)
        key = jax.random.key(seed)
        ks = jax.random.split(key, 5)
        s = 0.02
        return {'hidden_states': jax.random.normal(ks[0], (2, 256, H), dtype=jnp.float32), 'router_w': jax.random.normal(ks[1], (E, H), dtype=jnp.float32) * s, 'gate_w': jax.random.normal(ks[2], (E, I, H), dtype=jnp.float32) * s, 'up_w': jax.random.normal(ks[3], (E, I, H), dtype=jnp.float32) * s, 'down_w': jax.random.normal(ks[4], (E, H, I), dtype=jnp.float32) * s}
    _L0_ffn_all = _L0_ffn_setup()
    _L0_ffn_in = {k: v for k, v in _L0_ffn_all.items() if k in ('router_w', 'gate_w', 'up_w', 'down_w')}
    del _L0_ffn_all
    return {'x': x, 'L0_tok_W': _L0_tok_in['W'], 'L0_attn_wqkv': _L0_attn_in['wqkv'], 'L0_attn_wo': _L0_attn_in['wo'], 'L0_ffn_router_w': _L0_ffn_in['router_w'], 'L0_ffn_gate_w': _L0_ffn_in['gate_w'], 'L0_ffn_up_w': _L0_ffn_in['up_w'], 'L0_ffn_down_w': _L0_ffn_in['down_w']}

def reference(x, L0_tok_W, L0_attn_wqkv, L0_attn_wo, L0_ffn_router_w, L0_ffn_gate_w, L0_ffn_up_w, L0_ffn_down_w):
    import jax
    import jax.numpy as jnp

    def _L0_tok_ref(x, W):
        import jax, jax.numpy as jnp
        import numpy as np
        VOCAB = 50257
        D_MODEL = 256
        BATCH = 4
        SEQ = 1024
        return jnp.take(W, x, axis=0)

    def _L0_attn_ref(x, wqkv, wo):
        import jax, jax.numpy as jnp
        import numpy as np
        B, S, HID = (4, 256, 256)
        H, D = (16, 64)
        NEG_INF = -10000000000.0

        def rope_alternate(inputs, position, min_timescale=1.0, max_timescale=10000.0):
            d = inputs.shape[-1]
            half = d // 2
            fraction = 2.0 * jnp.arange(half, dtype=jnp.float32) / d
            timescale = min_timescale * (max_timescale / min_timescale) ** fraction
            sinusoid = position[:, :, None, None] / timescale
            sin, cos = (jnp.sin(sinusoid), jnp.cos(sinusoid))
            first, second = jnp.split(inputs, 2, axis=-1)
            return jnp.concatenate([(first * cos - second * sin).astype(inputs.dtype), (second * cos + first * sin).astype(inputs.dtype)], axis=-1)
        b, s, _ = x.shape
        qkv = jnp.einsum('bsh,hf->bsf', x, wqkv).reshape(b, s, 3, H, D)
        q, k, v = (qkv[:, :, 0], qkv[:, :, 1], qkv[:, :, 2])
        pos = jnp.broadcast_to(jnp.arange(s, dtype=jnp.float32)[None, :], (b, s))
        q = rope_alternate(q, pos)
        k = rope_alternate(k, pos)
        q = q / jnp.sqrt(jnp.float32(D)).astype(q.dtype)
        logits = jnp.einsum('bqhd,bkhd->bhqk', q, k)
        causal = jnp.where(jnp.tril(jnp.ones((s, s), dtype=bool))[None, None], 0.0, NEG_INF).astype(logits.dtype)
        probs = jax.nn.softmax(logits + causal, axis=-1)
        ctx = jnp.einsum('bhqk,bkhd->bqhd', probs, v).reshape(b, s, H * D)
        return jnp.einsum('bsf,fh->bsh', ctx, wo)

    def _L0_ffn_ref(hidden_states, router_w, gate_w, up_w, down_w):
        import jax, jax.numpy as jnp
        import numpy as np
        H = 256
        I = 704
        E = 8
        TOP_K = 2

        def _moe(hidden_states, router_w, gate_w, up_w, down_w):
            B, S, Hd = hidden_states.shape
            x = hidden_states.reshape(-1, Hd)
            logits = x @ router_w.T
            probs = jax.nn.softmax(logits.astype(jnp.float32), axis=-1)
            top_w, top_idx = jax.lax.top_k(probs, TOP_K)
            top_w = top_w.astype(x.dtype)
            onehot = jax.nn.one_hot(top_idx, E, dtype=x.dtype)
            w_te = jnp.einsum('tk,tke->te', top_w, onehot)
            g = jnp.einsum('th,eih->tei', x, gate_w)
            u = jnp.einsum('th,eih->tei', x, up_w)
            h = jax.nn.silu(g) * u
            y = jnp.einsum('tei,ehi,te->th', h, down_w, w_te)
            return y.reshape(B, S, Hd)
        return _moe(hidden_states, router_w, gate_w, up_w, down_w)
    h = _L0_tok_ref(x, L0_tok_W)
    h = h + _L0_attn_ref(_layernorm(h, axis=-1), L0_attn_wqkv, L0_attn_wo)
    h = h + _L0_ffn_ref(_layernorm(h, axis=-1), L0_ffn_router_w, L0_ffn_gate_w, L0_ffn_up_w, L0_ffn_down_w)
    return h

_drawn_inputs = setup_inputs


def setup_inputs(seed=0):
    import zlib

    import numpy as np

    out = dict(_drawn_inputs(seed))
    spreads = {}
    factors = {'L0_ffn_router_w': 8.0,
     'L0_ffn_gate_w': 7.995,
     'L0_ffn_up_w': 7.905,
     'L0_ffn_down_w': 7.898}
    for name, (base, spread) in spreads.items():
        noise = np.random.default_rng([zlib.crc32(name.encode()), seed]).standard_normal(out[name].shape)
        drawn = base * np.exp(spread * noise) if base else spread * noise
        out[name] = jnp.asarray(drawn.astype(out[name].dtype))
    for name, factor in factors.items():
        out[name] = (out[name] * factor).astype(out[name].dtype)
    return out
```

```python
from contextlib import ExitStack

import numpy as np

import concourse.bass as bass
from concourse import mybir

ALU = mybir.AluOpType
ACT = mybir.ActivationFunctionType
AX = mybir.AxisListType
F32 = mybir.dt.float32
F16 = mybir.dt.float16
BF16 = mybir.dt.bfloat16
I32 = mybir.dt.int32
U32 = mybir.dt.uint32

P = 128
B, S, DM = 2, 1024, 256
H, D = 16, 64
E, FF, TOPK = 8, 704, 2
T = B * S
NT = T // P
BT = S // P
KC = DM // P
NP_ = H // 2
NU = B * NP_
FC = -(-FF // P)
FH = FF // 2
SLOT_TILES = TOPK * T // P + E - 1
EPS = 1e-5
W_SCALE = 64.0
M_SCALE = 64.0
NEG = -1.0e10

PIECES = []
_col = 0
for _kt in range(BT):
    _q = _kt * P
    while _q < S:
        _n = min(512, S - _q)
        PIECES.append((_kt, _q, _n, _col))
        _q += _n
        _col += _n
PCOLS = _col
KT_COL = [min(c for kt, _, _, c in PIECES if kt == k) for k in range(BT)]
NPC = len(PIECES)
MPIECES = [(qt, hf, min(512, (qt + 1) * P - 512 * hf)) for qt in range(BT) for hf in range(1 if qt < 4 else 2)]
NMP = len(MPIECES)
PV_GROUPS = 2
Q_AT = [0, 3 * D]
K_AT = [5 * D, 8 * D]
HALVES = 11 * D
TP_USES = BT + 1 + 2


def slot_pieces(t):
    return range(NPC * t // BT, NPC * (t + 1) // BT)


def before_pack(n, t):
    return t if isinstance(n, int) and n == 0 else TP_USES * n - 2 + t


def before_maxima(n):
    return before_pack(n, BT)


def before_context(n, g):
    return (TP_USES * n + 2 * (BT + 1) if not (isinstance(n, int) and n == NU - 1) else TP_USES * n + BT + 1) + g


def program(nc, ids, emb, wqkv, wo, router, gate, up, down, rope_c, rope_s, out):
    xs = nc.dram_tensor("slot_x", (SLOT_TILES * P, DM), F32).ap()
    ys = nc.dram_tensor("slot_y", (SLOT_TILES * P, DM), F32).ap()
    top = ExitStack()
    with top:
        def sbt(ctx, name, shape, dt):
            return ctx.enter_context(nc.sbuf_tensor(name, shape, dt))

        def sem(ctx, name):
            return ctx.enter_context(nc.semaphore(name))

        h = sbt(top, "h", [P, NT, DM], F32)
        ident = sbt(top, "ident", [P, P], F32)
        stats = sbt(top, "stats", [P, 2, 6], F32)
        mv = sbt(top, "mv", [P, NT, 2], F32)
        veps = sbt(top, "veps", [P, NT], F32)
        std = sbt(top, "std", [P, NT], F32)
        rstd = sbt(top, "rstd", [P, NT], F32)
        banks = [top.enter_context(nc.psum_tensor(f"bank{i}", [P, 512], F32)) for i in range(8)]

        attention(nc, sbt, sem, h, ident, (stats, mv, veps, std, rstd), banks,
                  ids, emb, wqkv, wo, rope_c, rope_s, xs)
        experts(nc, sbt, sem, h, ident, (stats, mv, veps, std, rstd), banks,
                router, gate, up, down, xs, ys, out)


def layernorm_stats(nc, dve, act_ready, act_done, stat_done, h, norm):
    stats, mv, veps, std, rstd = norm
    for t in range(NT):
        nc.vector.bn_stats(stats[:, t % 2, :], h[:, t, :]).then_inc(stat_done, 1)
        dve.wait_ge(stat_done, 2 * t + 1)
        nc.vector.bn_aggr(mv[:, t, :], stats[:, t % 2, :]).then_inc(stat_done, 1)
    dve.wait_ge(stat_done, 2 * NT)
    nc.vector.tensor_scalar(veps[:], mv[:, :, 1], EPS, None, ALU.add).then_inc(act_ready, 1)
    dve.wait_ge(act_done, 1)
    nc.vector.reciprocal(rstd[:], std[:]).then_inc(stat_done, 1)
    dve.wait_ge(stat_done, 2 * NT + 1)


def attention(nc, sbt, sem, h, ident, norm, banks, ids, emb, wqkv, wo, rope_c, rope_s, xs):
    stats, mv, veps, std, rstd = norm
    ctx = ExitStack()
    with ctx:
        def sb(name, shape, dt):
            return sbt(ctx, name, shape, dt)

        def sm(name):
            return sem(ctx, name)

        ids_sb = sb("ids_sb", [P, NT], I32)
        ident16 = sb("ident16", [P, P], F16)
        identb = sb("identb", [P, P], BF16)
        mask_q = sb("mask_q", [P, P], BF16)
        mask_k = sb("mask_k", [P, P], BF16)
        maskf = sb("maskf", [P, 2, P], F32)
        zeros = sb("zeros", [P, DM], F32)
        xn = sb("xn", [P, 4, DM], F32)
        x16 = sb("x16", [P, 4, 2, DM], F16)
        xT = sb("xT", [P, 2, KC, T], F16)
        w16 = sb("w16", [P, 2, KC, NP_, 384], F16)
        wo_sb = sb("wo_sb", [P, NP_, DM], F32)
        rc = sb("rc", [P, BT, 4, D], F32)
        rs = sb("rs", [P, BT, 4, D], F32)
        rope_a = sb("rope_a", [P, 2, 4, D], F32)
        rope_b = sb("rope_b", [P, 2, 4, D], F32)
        roped = sb("roped", [P, 2, 4, D], F32)
        halves = sb("halves", [P, 2, HALVES], F16)
        stack = sb("stack", [P, B, 4, S], F16)
        aug = sb("aug", [65, B, 4, S], F16)
        v = sb("v", [P, B, BT, 2, D + 1], F32)
        probs = sb("probs", [P, 2, PCOLS], F32)
        mx = sb("mx", [P, 2, 16], F32)
        mneg = sb("mneg", [P, 2, 16], F32)
        m16 = sb("m16", [P, 16], F16)
        mT = sb("mT", [16, P], F16)
        rsum = sb("rsum", [P, 4], F32)
        cx = sb("cx", [P, BT, 2, D], F32)
        cT = sb("cT", [P, 2, 512], F32)

        w32 = probs[:, :, :].rearrange("p a c -> p (a c)")[:, 0:KC * NP_ * 384]
        w16hi = w16[:, 0].rearrange("p k u c -> p (k u c)")
        w16lo = w16[:, 1].rearrange("p k u c -> p (k u c)")
        xT_all = xT[:, :, :, :].rearrange("p a k t -> p (a k) t")

        qkv_ps = banks[0]
        tp_ps = banks[1]
        tp16 = tp_ps[:, :].bitcast(F16)
        max_ps = banks[2:4]
        st_ps = banks[4:6]
        ctx_ps = banks[6]
        y_ps = banks[7]

        s_ids, s_emb, s_zero, s_fill = sm("s_ids"), sm("s_emb"), sm("s_zero"), sm("s_fill")
        s_rope_tab, s_wqkv, s_wo = sm("s_rope_tab"), sm("s_wqkv"), sm("s_wo")
        s_c, s_const = sm("s_c"), sm("s_const")
        s_whi, s_wlo = sm("s_whi"), sm("s_wlo")
        s_stat, s_var, s_std = sm("s_stat"), sm("s_var"), sm("s_std")
        s_xn, s_xhi, s_xlo = sm("s_xn"), sm("s_xhi"), sm("s_xlo")
        s_xtp, s_xT = sm("s_xtp"), sm("s_xT")
        s_setup, pool_turn = sm("s_setup"), sm("pool_turn")
        qkv_ready, rope_terms, qkv_free = sm("qkv_ready"), sm("rope_terms"), sm("qkv_free")
        roped_ready, hi_ready, lo_ready = sm("roped_ready"), sm("hi_ready"), sm("lo_ready")
        pack_tp, max_tp, ctx_tp, tp_free = sm("pack_tp"), sm("max_tp"), sm("ctx_tp"), sm("tp_free")
        max_ready, max_free, mneg_ready, m16_ready = sm("max_ready"), sm("max_free"), sm("mneg_ready"), sm("m16_ready")
        mrow_ready = sm("mrow_ready")
        st_ready, st_free = sm("st_ready"), sm("st_free")
        pv_ready, rsum_ready, ctx_free = sm("pv_ready"), sm("rsum_ready"), sm("ctx_free")
        y_ready, y_free = sm("y_ready"), sm("y_free")

        block = ctx.enter_context(nc.Block())

        @block.sync
        def _(sp):
            sp.dma_start(ids_sb[:], ids).then_inc(s_ids, 16)
            sp.dma_start(w32, wqkv).then_inc(s_wqkv, 16)
            sp.dma_start(rc[:, :, :, :].rearrange("p t a d -> p (t a d)"), rope_c).then_inc(s_rope_tab, 16)
            sp.dma_start(rs[:, :, :, :].rearrange("p t a d -> p (t a d)"), rope_s).then_inc(s_rope_tab, 16)
            sp.dma_start(wo_sb[:, :, :].rearrange("p u n -> p (u n)"), wo).then_inc(s_wo, 16)
            sp.wait_ge(s_zero, 1)
            sp.dma_start(xs.rearrange("(p r) d -> p r d", r=SLOT_TILES),
                         zeros[:, :].unsqueeze(1).to_broadcast([P, SLOT_TILES, DM])).then_inc(s_fill, 16)

            def max_row(n, b):
                sp.wait_ge(tp_free, before_maxima(n) + 1)
                for hh in range(2):
                    sp.dma_start(aug[64:65, b, hh, :],
                                 mT[8 * hh:8 * hh + 8, :]).then_inc(mrow_ready, 16)

            max_row(0, 0)
            with sp.Fori(0, NP_ - 1) as p:
                max_row(2 * p + 1, 1)
                max_row(2 * p + 2, 0)
            max_row(NU - 1, 1)
            sp.wait_ge(s_fill, 16)

        @block.gpsimd
        def _(pool):
            nc.gpsimd.memset(zeros[:], 0.0).then_inc(s_zero, 1)
            pool.wait_ge(s_ids, 16)
            for t in range(NT):
                nc.gpsimd.indirect_dma_start(
                    out=h[:, t, :], out_offset=None, in_=emb,
                    in_offset=bass.IndirectOffsetOnAxis(ap=ids_sb[:, t:t + 1], axis=0)).then_inc(s_emb, 16)
            nc.gpsimd.memset(ident[:], 0.0).then_inc(s_c, 1)
            nc.gpsimd.memset(maskf[:], 0.0).then_inc(s_c, 1)
            pool.wait_ge(s_c, 2)
            nc.gpsimd.affine_select(out=ident[:], in_=ident[:], compare_op=ALU.not_equal, fill=1.0, base=0,
                                    pattern=[[-1, P]], channel_multiplier=1).then_inc(s_c, 1)
            nc.gpsimd.affine_select(out=maskf[:, 0, :], in_=maskf[:, 0, :], compare_op=ALU.is_ge, fill=NEG, base=0,
                                    pattern=[[-1, P]], channel_multiplier=1).then_inc(s_c, 1)
            nc.gpsimd.affine_select(out=maskf[:, 1, :], in_=maskf[:, 1, :], compare_op=ALU.is_ge, fill=NEG, base=0,
                                    pattern=[[1, P]], channel_multiplier=-1).then_inc(s_c, 1)
            pool.wait_ge(s_c, 5)
            nc.gpsimd.tensor_copy(ident16[:], ident[:]).then_inc(s_const, 1)
            nc.gpsimd.tensor_copy(identb[:], ident[:]).then_inc(s_const, 1)
            nc.gpsimd.tensor_copy(mask_q[:], maskf[:, 0, :]).then_inc(s_const, 1)
            nc.gpsimd.tensor_copy(mask_k[:], maskf[:, 1, :]).then_inc(s_const, 1)
            pool.sem_inc(s_xlo, 4)
            with pool.Fori(0, NT // 4) as g:
                for j in range(4):
                    pool.wait_ge(s_xhi, 4 * g + j + 1)
                    nc.gpsimd.tensor_tensor(x16[:, j, 1, :], xn[:, j, :], x16[:, j, 0, :],
                                            ALU.subtract).then_inc(s_xlo, 1)
            def split(n, t):
                i = t % 2
                pool.wait_ge(roped_ready, BT * n + t + 1)
                pool.sem_inc(pool_turn, 1)
                r = roped[:, i]
                hi = bass.AP(halves, HALVES * i, [[2 * HALVES, P], [5 * D, 2], [3 * D, 2], [1, D]])
                khi = bass.AP(halves, HALVES * i + K_AT[0] + D, [[2 * HALVES, P], [3 * D, 2], [1, D]])
                lo = bass.AP(halves, HALVES * i + D, [[2 * HALVES, P], [6 * D, 2], [3 * D, 2], [1, D]])
                hi4 = r.rearrange("p (a b) d -> p a b d", a=2)
                nc.gpsimd.tensor_copy(hi, hi4).then_inc(hi_ready, 1)
                nc.gpsimd.tensor_copy(khi, r[:, 2:4, :])
                pool.wait_ge(hi_ready, BT * n + t + 1)
                nc.gpsimd.tensor_tensor(lo, hi4, hi, ALU.subtract).then_inc(lo_ready, 1)

            for t in range(BT):
                split(0, t)
            with pool.Fori(0, NP_ - 1) as p:
                for t in range(BT):
                    split(2 * p + 1, t)
                for t in range(BT):
                    split(2 * p + 2, t)
            for t in range(BT):
                split(NU - 1, t)

        @block.scalar
        def _(act):
            act.wait_ge(s_wqkv, 16)
            nc.scalar.activation(w16hi, w32, ACT.Copy, scale=W_SCALE).then_inc(s_whi, 1)
            act.wait_ge(s_var, 1)
            nc.scalar.activation(std[:], veps[:], ACT.Sqrt).then_inc(s_std, 1)
            act.sem_inc(s_xT, 2)
            with act.Fori(0, NT // 4) as g:
                for j in range(4):
                    act.wait_ge(s_xn, 4 * g + j + 1)
                    nc.scalar.activation(x16[:, j, 0, :], xn[:, j, :], ACT.Copy).then_inc(s_xhi, 1)
                for j in range(4):
                    act.wait_ge(s_xtp, 4 * g + j + 1)
                    nc.scalar.activation(xT_all[:, :, bass.ds(512 * g + P * j, P)],
                                         banks[j % 2][:, :].bitcast(F16)[:, 0:512].rearrange("p (a t) -> p a t", a=4),
                                         ACT.Copy).then_inc(s_xT, 1)

            def value_copy(n, b, t):
                act.wait_ge(rope_terms, 2 * (BT * n + t) + 2)
                nc.scalar.activation(v[:, b, t, :, 0:D],
                                     qkv_ps[:, 256:384].rearrange("p (h d) -> p h d", h=2),
                                     ACT.Copy, scale=1.0 / W_SCALE).then_inc(qkv_free, 1)

            def stacks(n, b, t):
                act.wait_ge(pack_tp, BT * n + t + 1)
                nc.scalar.activation(stack[:, b, :, t * P:(t + 1) * P],
                                     tp16[:, 0:512].rearrange("p (a t) -> p a t", a=4), ACT.Copy)
                nc.scalar.activation(aug[0:64, b, :, t * P:(t + 1) * P],
                                     tp16[0:64, 256:768].rearrange("p (a t) -> p a t", a=4),
                                     ACT.Copy).then_inc(tp_free, 1)

            def exps(n, hh, j):
                kt, q, w, c = PIECES[j]
                act.wait_ge(st_ready, 2 * NPC * n + NPC * hh + j + 1)
                nc.scalar.activation(probs[:, hh, c:c + w], st_ps[j % 2][:, 0:w], ACT.Exp).then_inc(st_free, 1)

            def maxima(n):
                act.wait_ge(max_tp, n + 1)
                nc.scalar.activation(mT[:], tp16[0:16, 0:P], ACT.Copy).then_inc(tp_free, 1)

            def context(n, g):
                act.wait_ge(ctx_tp, 2 * n + g + 1)
                nc.scalar.activation(cT[:, g, :], tp_ps[:, :], ACT.Copy).then_inc(tp_free, 1)

            def unit(n, b, nxt):
                for t in range(BT + 1):
                    if nxt and t < BT:
                        value_copy(n + 1, 1 - b, t)
                    if t < BT:
                        for j in slot_pieces(t):
                            exps(n, 0, j)
                    if nxt and t > 0:
                        stacks(n + 1, 1 - b, t - 1)
                for j in range(NPC):
                    exps(n, 1, j)
                if nxt:
                    maxima(n + 1)
                for g in range(2):
                    context(n, g)

            act.sem_inc(st_free, 2)
            for t in range(BT + 1):
                if t < BT:
                    value_copy(0, 0, t)
                if t > 0:
                    stacks(0, 0, t - 1)
            maxima(0)
            with act.Fori(0, NP_ - 1) as p:
                unit(2 * p, 0, True)
                unit(2 * p + 1, 1, True)
            unit(NU - 2, 0, True)
            unit(NU - 1, 1, False)

        @block.tensor
        def _(pe):
            pe.wait_ge(s_const, 4)
            with pe.Fori(0, NT // 4) as g:
                for j in range(4):
                    pe.wait_ge(s_xlo, 4 + 4 * g + j + 1)
                    pe.wait_ge(s_xT, 4 * g + j + 1)
                    for a in range(4):
                        mm = nc.tensor.transpose(banks[j % 2][:, :].bitcast(F16)[:, a * P:(a + 1) * P],
                                                 x16[:, j, a // 2, (a % 2) * P:(a % 2 + 1) * P], ident16[:])
                    mm.then_inc(s_xtp, 1)
            pe.wait_ge(s_xT, NT + 2)
            pe.wait_ge(s_wlo, 1)

            def project(n, p, b, t):
                i = BT * n + t
                if not (isinstance(i, int) and i == 0):
                    pe.wait_ge(qkv_free, i)
                tok = S * b + P * t
                for kc in range(KC):
                    for a, c in ((0, 0), (0, 1), (1, 0)):
                        mm = nc.tensor.matmul(qkv_ps[:, 0:384], xT[:, a, kc, tok:tok + P],
                                              w16[:, c, kc, bass.ds(p, 1), :].rearrange("p o c -> p (o c)"),
                                              start=(kc == 0 and a == 0 and c == 0), stop=(kc == KC - 1 and a == 1))
                mm.then_inc(qkv_ready, 1)

            def pack(n, t):
                i = t % 2
                pe.wait_ge(lo_ready, BT * n + t + 1)
                w = before_pack(n, t)
                if not (isinstance(w, int) and w == 0):
                    pe.wait_ge(tp_free, w)
                for hh in range(2):
                    k, q = K_AT[hh], Q_AT[hh]
                    nc.tensor.transpose(tp16[:, hh * P:(hh + 1) * P], halves[:, i, k:k + 2 * D], ident16[:])
                    nc.tensor.transpose(tp16[:, (2 + hh) * P:(3 + hh) * P], halves[:, i, q:q + 2 * D], ident16[:])
                    mm = nc.tensor.transpose(tp16[0:D, (4 + hh) * P:(5 + hh) * P],
                                             halves[:, i, k + 2 * D:k + 3 * D], ident16[:])
                mm.then_inc(pack_tp, 1)

            def max_piece(n, b, hh, j):
                qt, hf, w = MPIECES[j]
                i = 2 * NMP * n + NMP * hh + j
                if not (isinstance(i, int) and i < 2):
                    pe.wait_ge(max_free, i - 1)
                pe.wait_ge(tp_free, before_pack(n, qt) + 1)
                diag = qt // 4 == hf
                ps = max_ps[j % 2]
                mm = nc.tensor.matmul(ps[:, 0:w], stack[:, b, 2 + hh, qt * P:(qt + 1) * P],
                                      stack[:, b, hh, 512 * hf:512 * hf + w], start=True, stop=not diag)
                if diag:
                    mm = nc.tensor.matmul(ps[:, w - P:w], identb[:], mask_q[:], start=False, stop=True)
                mm.then_inc(max_ready, 1)

            def max_rows(n):
                pe.wait_ge(m16_ready, n + 1)
                pe.wait_ge(tp_free, before_maxima(n))
                nc.tensor.transpose(tp16[0:16, 0:P], m16[:], ident16[:]).then_inc(max_tp, 1)

            def scores(n, b, hh, j):
                kt, q, w, c = PIECES[j]
                pe.wait_ge(st_free, 2 * NPC * n + NPC * hh + j + 1)
                ps = st_ps[j % 2]
                nc.tensor.matmul(ps[:, 0:w], stack[:, b, hh, kt * P:(kt + 1) * P], stack[:, b, 2 + hh, q:q + w],
                                 start=True, stop=False)
                mm = nc.tensor.matmul(ps[:, 0:w], aug[0:65, b, 2 + hh, kt * P:(kt + 1) * P],
                                      aug[0:65, b, hh, q:q + w], start=False, stop=(q != kt * P))
                if q == kt * P:
                    mm = nc.tensor.matmul(ps[:, 0:P], identb[:], mask_k[:], start=False, stop=True)
                mm.then_inc(st_ready, 1)

            def values(n, b, hh, g):
                pe.wait_ge(qkv_free, BT * (n + 1))
                pe.wait_ge(st_free, 2 + 2 * NPC * n + NPC * (hh + 1))
                pe.wait_ge(ctx_free, 4 * n + 2 * hh + g + 1)
                for qt in range(4 * g, 4 * g + 4):
                    for kt in range(qt + 1):
                        c = KT_COL[kt] + P * (qt - kt)
                        mm = nc.tensor.matmul(ctx_ps[:, (qt % 4) * 65:(qt % 4) * 65 + 65], probs[:, hh, c:c + P],
                                              v[:, b, kt, hh, :], start=(kt == 0), stop=(kt == qt))
                mm.then_inc(pv_ready, 1)

            def context(n, g):
                pe.wait_ge(ctx_free, 1 + 4 * n + 3 + g)
                pe.wait_ge(tp_free, before_context(n, g))
                for i in range(4):
                    mm = nc.tensor.transpose(tp_ps[:, i * P:(i + 1) * P],
                                             cx[:, 4 * g + i].rearrange("p h d -> p (h d)"), ident[:])
                mm.then_inc(ctx_tp, 1)

            def output(n, p, j):
                if j % 2 == 0:
                    pe.wait_ge(tp_free, before_context(n, j // 2) + 1)
                pe.wait_ge(y_free, 4 * n + j + 1)
                for i in range(2):
                    t = 2 * j + i
                    mm = nc.tensor.matmul(y_ps[:, i * DM:(i + 1) * DM], cT[:, t // 4, (t % 4) * P:(t % 4 + 1) * P],
                                          wo_sb[:, bass.ds(p, 1), :].rearrange("p o c -> p (o c)"),
                                          start=True, stop=True)
                mm.then_inc(y_ready, 1)

            def unit(n, p, b, nxt):
                pe.wait_ge(mrow_ready, 32 * (n + 1))
                for t in range(BT + 1):
                    if nxt and t < BT:
                        project(n + 1, p + b, 1 - b, t)
                    if t < BT:
                        for j in slot_pieces(t):
                            scores(n, b, 0, j)
                    if nxt and t > 0:
                        pack(n + 1, t - 1)
                for j in range(NPC):
                    scores(n, b, 1, j)
                    if nxt:
                        for i in (2 * j, 2 * j + 1):
                            max_piece(n + 1, 1 - b, i // NMP, i % NMP)
                    if j == 3:
                        values(n, b, 0, 0)
                    if j == 8:
                        values(n, b, 0, 1)
                values(n, b, 1, 0)
                if nxt:
                    max_rows(n + 1)
                values(n, b, 1, 1)
                context(n, 0)
                output(n, p, 0)
                output(n, p, 1)
                context(n, 1)
                output(n, p, 2)
                output(n, p, 3)

            for t in range(BT + 1):
                if t < BT:
                    project(0, 0, 0, t)
                if t > 0:
                    pack(0, t - 1)
            for i in range(2 * NMP):
                max_piece(0, 0, i // NMP, i % NMP)
            max_rows(0)
            pe.wait_ge(s_setup, 3)
            pe.wait_ge(s_wo, 16)
            with pe.Fori(0, NP_ - 1) as p:
                unit(2 * p, p, 0, True)
                unit(2 * p + 1, p, 1, True)
            unit(NU - 2, NP_ - 1, 0, True)
            unit(NU - 1, NP_ - 1, 1, False)

        @block.vector
        def _(dve):
            nc.vector.memset(aug[64:65, :, 2:4, :], M_SCALE).then_inc(s_setup, 1)
            nc.vector.memset(v[:, :, :, :, D:D + 1], 1.0).then_inc(s_setup, 1)
            nc.vector.memset(mx[:, 1, :], -3.0e38).then_inc(s_setup, 1)
            dve.wait_ge(s_setup, 3)
            dve.wait_ge(s_emb, 16 * NT)
            layernorm_stats(nc, dve, s_var, s_std, s_stat, h, norm)
            with dve.Fori(0, NT // 4) as g:
                for j in range(4):
                    t = 4 * g + j
                    dve.wait_ge(s_xlo, t + 1)
                    nc.vector.tensor_scalar(xn[:, j, :], h[:, bass.ds(t, 1), :].rearrange("p o c -> p (o c)"),
                                            mv[:, bass.ds(t, 1), 0], rstd[:, bass.ds(t, 1)],
                                            ALU.subtract, ALU.mult).then_inc(s_xn, 1)
            dve.wait_ge(s_whi, 1)
            nc.vector.scalar_tensor_tensor(w16lo, w32, W_SCALE, w16hi, ALU.mult, ALU.subtract).then_inc(s_wlo, 1)
            dve.wait_ge(s_rope_tab, 32)

            def rotate(n, t):
                i = t % 2
                g = BT * n + t
                dve.wait_ge(qkv_ready, g + 1)
                qk = qkv_ps[:, 0:256].rearrange("p (a d) -> p a d", a=4)
                nc.vector.tensor_tensor(rope_a[:, i], qk, rc[:, t], ALU.mult).then_inc(rope_terms, 1)
                swapped = bass.AP(qkv_ps, D // 2, [[512, P], [D, 4], [-(D // 2), 2], [1, D // 2]])
                nc.vector.tensor_tensor(rope_b[:, i].rearrange("p a (s d) -> p a s d", s=2), swapped,
                                        rs[:, t].rearrange("p a (s d) -> p a s d", s=2),
                                        ALU.mult).then_inc(rope_terms, 1)
                dve.wait_ge(rope_terms, 2 * g + 2)
                if not (isinstance(g, int) and g < 2):
                    dve.wait_ge(lo_ready, g - 1)
                nc.vector.tensor_tensor(roped[:, i], rope_a[:, i], rope_b[:, i], ALU.add).then_inc(roped_ready, 1)

            def maximum(n, hh, j):
                qt, hf, w = MPIECES[j]
                dve.wait_ge(max_ready, 2 * NMP * n + NMP * hh + j + 1)
                nc.vector.reduce_max(mx[:, hf, 8 * hh + qt:8 * hh + qt + 1], max_ps[j % 2][:, 0:w],
                                     AX.X).then_inc(max_free, 1)

            def negate(n):
                dve.wait_ge(max_free, 2 * NMP * (n + 1))
                nc.vector.tensor_scalar(mneg[:], mx[:], -1.0 / M_SCALE, None, ALU.mult).then_inc(mneg_ready, 1)
                dve.wait_ge(mneg_ready, n + 1)
                nc.vector.tensor_tensor(m16[:], mneg[:, 0, :], mneg[:, 1, :], ALU.min).then_inc(m16_ready, 1)

            def normalize(n, hh, g):
                i = 4 * n + 2 * hh + g
                acc = ctx_ps[:, 0:260].rearrange("p (q d) -> p q d", q=4)
                dve.wait_ge(pv_ready, i + 1)
                nc.vector.reciprocal(rsum[:], acc[:, :, D]).then_inc(rsum_ready, 1)
                dve.wait_ge(rsum_ready, i + 1)
                nc.vector.tensor_tensor(cx[:, 4 * g:4 * g + 4, hh, :], acc[:, :, 0:D],
                                        rsum[:, :].unsqueeze(2).to_broadcast([P, 4, D]),
                                        ALU.mult).then_inc(ctx_free, 1)

            def residual(n, b, j):
                dve.wait_ge(y_ready, 4 * n + j + 1)
                rows = h[:, BT * b + 2 * j:BT * b + 2 * j + 2, :]
                nc.vector.tensor_tensor(rows, y_ps[:, :].rearrange("p (t c) -> p t c", t=2), rows,
                                        ALU.add).then_inc(y_free, 1)

            def unit(n, b, nxt):
                if nxt:
                    for t in range(BT):
                        rotate(n + 1, t)
                for j in range(NPC):
                    if nxt:
                        for i in (2 * j, 2 * j + 1):
                            maximum(n + 1, i // NMP, i % NMP)
                    if j == 4:
                        normalize(n, 0, 0)
                    if j == 9:
                        normalize(n, 0, 1)
                if nxt:
                    negate(n + 1)
                normalize(n, 1, 0)
                normalize(n, 1, 1)
                for j in range(4):
                    residual(n, b, j)

            dve.sem_inc(ctx_free, 1)
            dve.sem_inc(y_free, 1)
            for t in range(BT):
                rotate(0, t)
            for i in range(2 * NMP):
                maximum(0, i // NMP, i % NMP)
            negate(0)
            with dve.Fori(0, NP_ - 1) as p:
                unit(2 * p, 0, True)
                unit(2 * p + 1, 1, True)
            unit(NU - 2, 0, True)
            unit(NU - 1, 1, False)


def experts(nc, sbt, sem, h, ident, norm, banks, router, gate, up, down, xs, ys, out):
    stats, mv, veps, std, rstd = norm
    ctx = ExitStack()
    with ctx:
        pos = sbt(ctx, "pos", [P, TOPK, NT], I32)
        gates = sbt(ctx, "gates", [P, NT, 8], F32)
        tile_expert = sbt(ctx, "tile_expert", [1, SLOT_TILES], I32)
        gate_sb = sbt(ctx, "gate_sb", [P, E, KC, FF], F32)
        up_sb = sbt(ctx, "up_sb", [P, E, KC, FF], F32)
        down_sb = sbt(ctx, "down_sb", [P, E, FC, DM], F32)
        weights_in = sem(ctx, "weights_in")
        tail_zero = sem(ctx, "tail_zero")
        with ExitStack() as c:
            route(nc, c, sbt, sem, h, ident, norm, banks, router, gate, up, down, xs,
                  pos, gates, tile_expert, gate_sb, up_sb, down_sb, weights_in, tail_zero)
        with ExitStack() as c:
            feed_forward(nc, c, sbt, sem, ident, banks, xs, ys, tile_expert, gate_sb, up_sb, down_sb,
                         weights_in, tail_zero)
        with ExitStack() as c:
            combine(nc, c, sbt, sem, h, ys, pos, gates, out)


def route(nc, ctx, sbt, sem, h, ident, norm, banks, router, gate, up, down, xs,
          pos, gates, tile_expert, gate_sb, up_sb, down_sb, weights_in, tail_zero):
    stats, mv, veps, std, rstd = norm

    def sb(name, shape, dt):
        return sbt(ctx, name, shape, dt)

    def sm(name):
        return sem(ctx, name)

    xn = sb("xn2", [P, NT, DM], F32)
    xT = sb("xT2", [P, 2, KC, P], F32)
    router_sb = sb("router_sb", [P, KC, E], F32)
    logits = sb("logits", [P, NT, E], F32)
    shifted = sb("shifted", [P, NT, E], F32)
    expd = sb("expd", [P, NT, E], F32)
    rmax = sb("rmax", [P, NT], F32)
    total = sb("total", [P, NT], F32)
    inv = sb("inv", [P, NT], F32)
    pr = sb("pr", [P, NT, E], F32)
    idx = sb("idx", [P, NT, 8], U32)
    idxf = sb("idxf", [P, NT, 2], F32)
    iota_e = sb("iota_e", [P, E], F32)
    iota_t = sb("iota_t", [1, SLOT_TILES], F32)
    before = sb("before", [P, P], F32)
    ones = sb("ones", [P, P], F32)
    hot = sb("hot", [P, TOPK, NT, E], F32)
    chosen = sb("chosen", [P, NT, E], F32)
    cum = sb("cum", [P, 2, NT, E], F32)
    rank = sb("rank", [P, NT, E], F32)
    cnt_i = sb("cnt_i", [P, E], I32)
    cnt_s = sb("cnt_s", [P, E], I32)
    tiles = sb("tiles", [P, E], F32)
    ecum = sb("ecum", [P, 2, E], F32)
    base = sb("base", [P, E], F32)
    picked = sb("picked", [P, TOPK, NT, E], F32)
    posf = sb("posf", [P, TOPK, NT], F32)
    past = sb("past", [1, SLOT_TILES, E], F32)
    texp = sb("texp", [1, SLOT_TILES], F32)

    c_made, c_sel = sm("c_made"), sm("c_sel")
    r_in = sm("r_in")
    stat, var, root = sm("stat"), sm("var"), sm("root")
    xn_ready, xtp, xt_ready, lg_ready = sm("xn_ready2"), sm("xtp2"), sm("xt_ready2"), sm("lg_ready2")
    sh_ready, ex_ready = sm("sh_ready"), sm("ex_ready")
    chosen_ready, ranks_ready, step_done, pos_ready = sm("chosen_ready"), sm("ranks_ready"), sm("step_done"), sm("pos_ready")
    scattered = sm("scattered")

    block = ctx.enter_context(nc.Block())

    @block.sync
    def _(sp):
        sp.dma_start(router_sb[:, :, :].rearrange("p k e -> p (k e)"), router).then_inc(r_in, 16)
        for e in range(E):
            sp.dma_start(gate_sb[:, e].rearrange("p k f -> p (k f)"), gate[e]).then_inc(weights_in, 16)
            sp.dma_start(up_sb[:, e].rearrange("p k f -> p (k f)"), up[e]).then_inc(weights_in, 16)
            sp.dma_start(down_sb[:, e, 0:FF // P, :],
                         down[e, 0:FF // P * P, :].rearrange("(c p) d -> p c d", p=P)).then_inc(weights_in, 16)
            sp.dma_start(down_sb[0:FF % P, e, FC - 1, :], down[e, FF // P * P:FF, :]).then_inc(weights_in, 16)

    @block.gpsimd
    def _(pool):
        nc.gpsimd.memset(down_sb[FF % P:P, :, FC - 1, :], 0.0).then_inc(tail_zero, 1)
        pool.wait_ge(tail_zero, 1)
        nc.gpsimd.iota(iota_e[:], pattern=[[1, E]], base=0, channel_multiplier=0,
                       allow_small_or_imprecise_dtypes=True).then_inc(c_made, 1)
        nc.gpsimd.iota(iota_t[:], pattern=[[1, SLOT_TILES]], base=0, channel_multiplier=0,
                       allow_small_or_imprecise_dtypes=True).then_inc(c_made, 1)
        nc.gpsimd.memset(ones[:], 1.0).then_inc(c_sel, 1)
        pool.wait_ge(c_sel, 1)
        nc.gpsimd.affine_select(out=before[:], in_=ones[:], compare_op=ALU.is_gt, fill=0.0, base=0,
                                pattern=[[1, P]], channel_multiplier=-1).then_inc(c_made, 1)
        pool.wait_ge(pos_ready, 1)
        for k in range(TOPK):
            for t in range(NT):
                nc.gpsimd.indirect_dma_start(
                    out=xs, out_offset=bass.IndirectOffsetOnAxis(ap=pos[:, k, t:t + 1], axis=0),
                    in_=xn[:, t, :], in_offset=None).then_inc(scattered, 16)
        pool.wait_ge(scattered, 16 * TOPK * NT)

    @block.scalar
    def _(act):
        act.wait_ge(var, 1)
        nc.scalar.activation(std[:], veps[:], ACT.Sqrt).then_inc(root, 1)
        for t in range(NT):
            act.wait_ge(xtp, t + 1)
            nc.scalar.activation(xT[:, t % 2].rearrange("p k t -> p (k t)"), banks[t % 2][:, 0:KC * P],
                                 ACT.Copy).then_inc(xt_ready, 1)
        act.wait_ge(sh_ready, 1)
        nc.scalar.activation(expd[:], shifted[:], ACT.Exp).then_inc(ex_ready, 1)

    @block.tensor
    def _(pe):
        pe.wait_ge(r_in, 16)

        def logit(t):
            pe.wait_ge(xt_ready, t + 1)
            for kc in range(KC):
                mm = nc.tensor.matmul(banks[2][:, t * E:(t + 1) * E], xT[:, t % 2, kc, :], router_sb[:, kc, :],
                                      start=(kc == 0), stop=(kc == KC - 1))
            mm.then_inc(lg_ready, 1)

        for t in range(NT):
            pe.wait_ge(xn_ready, t + 1)
            if t >= 2:
                pe.wait_ge(xt_ready, t - 1)
            for kc in range(KC):
                mm = nc.tensor.transpose(banks[t % 2][:, kc * P:(kc + 1) * P], xn[:, t, kc * P:(kc + 1) * P], ident[:])
            mm.then_inc(xtp, 1)
            if t >= 1:
                logit(t - 1)
        logit(NT - 1)
        pe.wait_ge(chosen_ready, 1)
        pe.wait_ge(c_made, 3)
        flat = chosen[:, :, :].rearrange("p t e -> p (t e)")
        nc.tensor.matmul(banks[3][:, 0:NT * E], before[:], flat, start=True, stop=True)
        nc.tensor.matmul(banks[4][:, 0:NT * E], ones[:], flat, start=True, stop=True).then_inc(ranks_ready, 1)

    @block.vector
    def _(dve):
        done = [0]

        def step(ins):
            done[0] += 1
            ins.then_inc(step_done, 1)
            dve.wait_ge(step_done, done[0])

        layernorm_stats(nc, dve, var, root, stat, h, norm)
        for t in range(NT):
            nc.vector.tensor_scalar(xn[:, t, :], h[:, t, :], mv[:, t, 0:1], rstd[:, t:t + 1],
                                    ALU.subtract, ALU.mult).then_inc(xn_ready, 1)
        dve.wait_ge(lg_ready, NT)
        step(nc.vector.tensor_copy(logits[:, :, :].rearrange("p t e -> p (t e)"), banks[2][:, 0:NT * E]))
        step(nc.vector.reduce_max(rmax[:], logits[:], AX.X))
        nc.vector.tensor_tensor(shifted[:], logits[:], rmax[:, :].unsqueeze(2).to_broadcast([P, NT, E]),
                                ALU.subtract).then_inc(sh_ready, 1)
        dve.wait_ge(ex_ready, 1)
        step(nc.vector.reduce_sum(total[:], expd[:], AX.X))
        step(nc.vector.reciprocal(inv[:], total[:]))
        step(nc.vector.tensor_tensor(pr[:], expd[:], inv[:, :].unsqueeze(2).to_broadcast([P, NT, E]), ALU.mult))
        for t in range(NT):
            last = nc.vector.max(gates[:, t, :], pr[:, t, :])
        step(last)
        for t in range(NT):
            last = nc.vector.max_index(idx[:, t, :], gates[:, t, :], pr[:, t, :])
        step(last)
        step(nc.vector.tensor_copy(idxf[:], idx[:, :, 0:2]))
        dve.wait_ge(c_made, 3)
        for k in range(TOPK):
            last = nc.vector.tensor_tensor(hot[:, k], iota_e[:, :].unsqueeze(1).to_broadcast([P, NT, E]),
                                           idxf[:, :, k].unsqueeze(2).to_broadcast([P, NT, E]), ALU.is_equal)
        step(last)
        nc.vector.tensor_tensor(chosen[:], hot[:, 0], hot[:, 1], ALU.add).then_inc(chosen_ready, 1)
        dve.wait_ge(ranks_ready, 1)
        tile_cnt = banks[4][:, 0:NT * E].rearrange("p (t e) -> p t e", e=E)
        step(nc.vector.tensor_copy(cum[:, 0], tile_cnt))
        a, d = 0, 1
        while d < NT:
            nc.vector.tensor_copy(cum[:, 1 - a, 0:d, :], cum[:, a, 0:d, :])
            step(nc.vector.tensor_tensor(cum[:, 1 - a, d:NT, :], cum[:, a, d:NT, :], cum[:, a, 0:NT - d, :], ALU.add))
            a, d = 1 - a, 2 * d
        step(nc.vector.tensor_scalar(cnt_i[:], cum[:, a, NT - 1, :], float(P - 1), None, ALU.add))
        step(nc.vector.tensor_scalar(cnt_s[:], cnt_i[:], 7, None, ALU.arith_shift_right))
        step(nc.vector.tensor_copy(tiles[:], cnt_s[:]))
        step(nc.vector.tensor_copy(ecum[:, 0], tiles[:]))
        ea, d = 0, 1
        while d < E:
            nc.vector.tensor_copy(ecum[:, 1 - ea, 0:d], ecum[:, ea, 0:d])
            step(nc.vector.tensor_tensor(ecum[:, 1 - ea, d:E], ecum[:, ea, d:E], ecum[:, ea, 0:E - d], ALU.add))
            ea, d = 1 - ea, 2 * d
        step(nc.vector.tensor_tensor(base[:], ecum[:, ea], tiles[:], ALU.subtract))
        step(nc.vector.tensor_tensor(rank[:], cum[:, a], tile_cnt, ALU.subtract))
        step(nc.vector.tensor_tensor(rank[:], banks[3][:, 0:NT * E].rearrange("p (t e) -> p t e", e=E), rank[:], ALU.add))
        step(nc.vector.tensor_scalar(base[:], base[:], float(P), None, ALU.mult))
        step(nc.vector.tensor_tensor(rank[:], rank[:], base[:, :].unsqueeze(1).to_broadcast([P, NT, E]), ALU.add))
        for k in range(TOPK):
            last = nc.vector.tensor_tensor(picked[:, k], hot[:, k], rank[:], ALU.mult)
        step(last)
        step(nc.vector.reduce_sum(posf[:], picked[:], AX.X))
        nc.vector.tensor_copy(pos[:], posf[:]).then_inc(pos_ready, 1)
        step(nc.vector.tensor_tensor(past[:], iota_t[:, :].unsqueeze(2).to_broadcast([1, SLOT_TILES, E]),
                                     ecum[0:1, ea].unsqueeze(1).to_broadcast([1, SLOT_TILES, E]), ALU.is_ge))
        step(nc.vector.reduce_sum(texp[:], past[:], AX.X))
        step(nc.vector.tensor_scalar(tile_expert[:], texp[:], float(E - 1), None, ALU.min))


def feed_forward(nc, ctx, sbt, sem, ident, banks, xs, ys, tile_expert, gate_sb, up_sb, down_sb,
                 weights_in, tail_zero):
    def sb(name, shape, dt):
        return sbt(ctx, name, shape, dt)

    def sm(name):
        return sem(ctx, name)

    x_in = sb("x_in", [P, 2, DM], F32)
    xT = sb("xT3", [P, 2, KC, P], F32)
    sg = sb("sg", [P, FF], F32)
    hh = sb("hh", [P, FC * P], F32)
    hT = sb("hT", [P, FC, P], F32)
    y_sb = sb("y_sb", [P, 2, DM], F32)

    x_loaded = [sm("x_loaded0"), sm("x_loaded1")]
    y_stored = [sm("y_stored0"), sm("y_stored1")]
    pad_zero, xt_tp, xt_ready = sm("pad_zero"), sm("xt_tp"), sm("xt_ready")
    g_ready, u_ready, sg_ready, hh_ready = sm("g_ready"), sm("u_ready"), sm("sg_ready"), sm("hh_ready")
    ht_tp, ht_ready, y_ready, y_free = sm("ht_tp"), sm("ht_ready"), sm("y_ready3"), sm("y_free3")

    xt_ps = banks[0]
    y_ps = banks[1]
    ht_ps = banks[2:4]
    g_ps = banks[4:6]
    u_ps = banks[6:8]
    n_loops = (SLOT_TILES - 1) // 2
    assert SLOT_TILES == 2 * n_loops + 1

    block = ctx.enter_context(nc.Block())

    @block.sync
    def _(sp):
        def load(j, b):
            sp.dma_start(x_in[:, b, :], xs[bass.ds(j * P, P), :]).then_inc(x_loaded[b], 16)

        def store(j, b):
            sp.wait_ge(y_free, j + 2)
            sp.dma_start(ys[bass.ds(j * P, P), :], y_sb[:, b, :]).then_inc(y_stored[b], 16)

        sp.sem_inc(y_stored[0], 16)
        sp.sem_inc(y_stored[1], 16)
        load(0, 0)
        load(1, 1)
        with sp.Fori(0, n_loops - 1) as i:
            for b in range(2):
                j = 2 * i + b
                sp.wait_ge(xt_tp, j + 1)
                load(j + 2, b)
                store(j, b)
        sp.wait_ge(xt_tp, SLOT_TILES - 2)
        load(SLOT_TILES - 1, 0)
        for j in range(SLOT_TILES - 3, SLOT_TILES):
            store(j, j % 2)
        sp.wait_ge(y_stored[0], 16 + 16 * (n_loops + 1))
        sp.wait_ge(y_stored[1], 16 + 16 * n_loops)

    @block.scalar
    def _(act):
        def silu(j):
            act.wait_ge(g_ready, j + 1)
            for c in range(2):
                last = nc.scalar.activation(sg[:, c * FH:(c + 1) * FH], g_ps[c][:, 0:FH], ACT.Silu)
            last.then_inc(sg_ready, 1)

        def hidden_copy(j):
            act.wait_ge(ht_tp, j + 1)
            nc.scalar.activation(hT[:, 0:4, :].rearrange("p c t -> p (c t)"), ht_ps[0][:, :], ACT.Copy)
            nc.scalar.activation(hT[:, 4:FC, :].rearrange("p c t -> p (c t)"), ht_ps[1][:, 0:(FC - 4) * P],
                                 ACT.Copy).then_inc(ht_ready, 1)

        silu(0)
        with act.Fori(0, n_loops) as i:
            for b in range(2):
                j = 2 * i + 1 + b
                hidden_copy(j - 1)
                silu(j)
        hidden_copy(SLOT_TILES - 1)

    @block.vector
    def _(dve):
        def x_copy(j, b):
            dve.wait_ge(xt_tp, j + 1)
            nc.vector.tensor_copy(xT[:, b].rearrange("p k t -> p (k t)"), xt_ps[:, 0:KC * P]).then_inc(xt_ready, 1)

        def gated(j):
            dve.wait_ge(sg_ready, j + 1)
            dve.wait_ge(u_ready, j + 1)
            for c in range(2):
                last = nc.vector.tensor_tensor(hh[:, c * FH:(c + 1) * FH], u_ps[c][:, 0:FH],
                                               sg[:, c * FH:(c + 1) * FH], ALU.mult)
            last.then_inc(hh_ready, 1)

        def y_copy(j, b):
            dve.wait_ge(y_ready, j + 1)
            dve.wait_ge(y_stored[b], 16 * (j // 2 + 1) if isinstance(j, int) else 16 * y_index[0] + 16)
            nc.vector.tensor_copy(y_sb[:, b, :], y_ps[:, 0:DM]).then_inc(y_free, 1)

        y_index = [0]
        nc.vector.memset(hh[:, FF:FC * P], 0.0).then_inc(pad_zero, 1)
        dve.sem_inc(y_free, 1)
        x_copy(0, 0)
        gated(0)
        with dve.Fori(0, n_loops) as i:
            y_index[0] = i
            for b in range(2):
                j = 2 * i + 1 + b
                x_copy(j, 1 - b)
                gated(j)
                y_copy(j - 1, b)
        y_copy(SLOT_TILES - 1, 0)

    @block.tensor
    def _(pe):
        pe.wait_ge(weights_in, 16 * 4 * E)
        pe.wait_ge(tail_zero, 1)
        pe.wait_ge(pad_zero, 1)

        def x_transpose(j, b, i):
            pe.wait_ge(x_loaded[b], 16 * (i + 1))
            if not isinstance(j, int):
                pe.wait_ge(xt_ready, j)
            for kc in range(KC):
                mm = nc.tensor.transpose(xt_ps[:, kc * P:(kc + 1) * P], x_in[:, b, kc * P:(kc + 1) * P], ident[:])
            mm.then_inc(xt_tp, 1)

        def gate_up(j, b):
            e = nc.tensor.value_load(tile_expert[0:1, bass.ds(j, 1)], min_val=0, max_val=E - 1)
            pe.wait_ge(xt_ready, j + 1)
            for w, ps, ready in ((gate_sb, g_ps, g_ready), (up_sb, u_ps, u_ready)):
                for c in range(2):
                    for kc in range(KC):
                        mm = nc.tensor.matmul(ps[c][:, 0:FH], xT[:, b, kc, :],
                                              w[:, bass.ds(e, 1), kc, c * FH:(c + 1) * FH].rearrange("p o f -> p (o f)"),
                                              start=(kc == 0), stop=(kc == KC - 1))
                mm.then_inc(ready, 1)
            return e

        def hidden_transpose(j):
            pe.wait_ge(hh_ready, j + 1)
            for c in range(FC):
                mm = nc.tensor.transpose(ht_ps[c // 4][:, (c % 4) * P:(c % 4 + 1) * P], hh[:, c * P:(c + 1) * P], ident[:])
            mm.then_inc(ht_tp, 1)

        def down_proj(j):
            e = nc.tensor.value_load(tile_expert[0:1, bass.ds(j, 1)], min_val=0, max_val=E - 1)
            pe.wait_ge(ht_ready, j + 1)
            pe.wait_ge(y_free, j + 1)
            for c in range(FC):
                mm = nc.tensor.matmul(y_ps[:, 0:DM], hT[:, c, :],
                                      down_sb[:, bass.ds(e, 1), c, :].rearrange("p o d -> p (o d)"),
                                      start=(c == 0), stop=(c == FC - 1))
            mm.then_inc(y_ready, 1)

        x_transpose(0, 0, 0)
        gate_up(0, 0)
        with pe.Fori(0, n_loops) as i:
            for b in range(2):
                j = 2 * i + 1 + b
                x_transpose(j, 1 - b, i + b)
                hidden_transpose(j - 1)
                gate_up(j, 1 - b)
                down_proj(j - 1)
        hidden_transpose(SLOT_TILES - 1)
        down_proj(SLOT_TILES - 1)


def combine(nc, ctx, sbt, sem, h, ys, pos, gates, out):
    RING = 4
    y = sbt(ctx, "y_pair", [P, RING, TOPK, DM], F32)
    y_in = [sem(ctx, f"y_in{r}") for r in range(RING)]
    added, first, stored = sem(ctx, "added"), sem(ctx, "first"), sem(ctx, "stored")
    block = ctx.enter_context(nc.Block())

    @block.gpsimd
    def _(pool):
        for t in range(NT):
            if t >= RING:
                pool.wait_ge(added, t - RING + 1)
            for k in range(TOPK):
                nc.gpsimd.indirect_dma_start(
                    out=y[:, t % RING, k, :], out_offset=None, in_=ys,
                    in_offset=bass.IndirectOffsetOnAxis(ap=pos[:, k, t:t + 1], axis=0)).then_inc(y_in[t % RING], 16)

    @block.vector
    def _(dve):
        for t in range(NT):
            dve.wait_ge(y_in[t % RING], 32 * (t // RING + 1))
            nc.vector.scalar_tensor_tensor(h[:, t, :], y[:, t % RING, 0, :], gates[:, t, 0:1], h[:, t, :],
                                           ALU.mult, ALU.add).then_inc(first, 1)
            dve.wait_ge(first, t + 1)
            nc.vector.scalar_tensor_tensor(h[:, t, :], y[:, t % RING, 1, :], gates[:, t, 1:2], h[:, t, :],
                                           ALU.mult, ALU.add).then_inc(added, 1)

    @block.sync
    def _(sp):
        for t in range(NT):
            sp.wait_ge(added, t + 1)
            sp.dma_start(out[t * P:(t + 1) * P, :], h[:, t, :]).then_inc(stored, 16)
        sp.wait_ge(stored, 16 * NT)


def rope_tables():
    half = D // 2
    fraction = (np.float32(2.0) * np.arange(half, dtype=np.float32) / np.float32(D)).astype(np.float32)
    timescale = (np.float32(10000.0) ** fraction).astype(np.float32)
    angle = (np.arange(S, dtype=np.float32)[:, None] / timescale).astype(np.float32)
    sin, cos = np.sin(angle), np.cos(angle)
    scale = np.array([D ** -0.5, D ** -0.5, 1.0, 1.0], np.float32) / np.float32(W_SCALE)

    def lay(a):
        a = (a[:, None, :] * scale[None, :, None]).astype(np.float32)
        return np.ascontiguousarray(a.reshape(BT, P, 4, D).transpose(1, 0, 2, 3)).reshape(P, BT * 4 * D)

    return lay(np.concatenate([cos, cos], 1)), lay(np.concatenate([-sin, sin], 1))


def kernel(x, L0_tok_W, L0_attn_wqkv, L0_attn_wo, L0_ffn_router_w, L0_ffn_gate_w, L0_ffn_up_w, L0_ffn_down_w):
    import concourse.bacc as _bacc
    from concourse.bass_utils import run_bass_kernel_spmd as _run

    rope_c, rope_s = rope_tables()
    wqkv = np.asarray(L0_attn_wqkv).reshape(KC, P, 3, NP_, 128).transpose(1, 0, 3, 2, 4)

    def up_layout(w):
        return np.asarray(w).transpose(0, 2, 1).reshape(E, KC, P, FF).transpose(0, 2, 1, 3).reshape(E, P, KC * FF)

    arrays = {
        "ids": np.asarray(x).reshape(NT, P).T,
        "emb": np.asarray(L0_tok_W),
        "wqkv": wqkv.reshape(P, KC * NP_ * 384),
        "wo": np.asarray(L0_attn_wo).reshape(NP_, P, DM).transpose(1, 0, 2).reshape(P, NP_ * DM),
        "router": np.asarray(L0_ffn_router_w).T.reshape(KC, P, E).transpose(1, 0, 2).reshape(P, KC * E),
        "gate": up_layout(L0_ffn_gate_w),
        "up": up_layout(L0_ffn_up_w),
        "down": np.asarray(L0_ffn_down_w).transpose(0, 2, 1),
        "rope_c": rope_c,
        "rope_s": rope_s,
    }
    arrays = {name: np.ascontiguousarray(a) for name, a in arrays.items()}
    nc = _bacc.Bacc("TRN2", target_bir_lowering=False, num_devices=1)
    args = [nc.dram_tensor(name, a.shape, mybir.dt.from_np(a.dtype), kind="ExternalInput").ap()
            for name, a in arrays.items()]
    out = nc.dram_tensor("out", (T, DM), F32, kind="ExternalOutput").ap()
    program(nc, *args, out)
    r = _run(nc, [arrays], core_ids=[0])
    return r.results[0]["out"].reshape(B, S, DM)
```

```python
from contextlib import ExitStack

import numpy as np

import concourse.bass as bass
from concourse import mybir

ALU = mybir.AluOpType
ACT = mybir.ActivationFunctionType
AX = mybir.AxisListType
F32 = mybir.dt.float32
F16 = mybir.dt.float16
BF16 = mybir.dt.bfloat16
I32 = mybir.dt.int32
U32 = mybir.dt.uint32

P = 128
B, S, DM = 2, 1024, 256
H, D = 16, 64
E, FF, TOPK = 8, 704, 2
T = B * S
NT = T // P
BT = S // P
KC = DM // P
NP_ = H // 2
NU = B * NP_
FC = -(-FF // P)
FH = FF // 2
SLOT_TILES = TOPK * T // P + E - 1
EPS = 1e-5
W_SCALE = 64.0
M_SCALE = 64.0
NEG = -1.0e10

PIECES = []
_col = 0
for _half in range(2):
    for _kt in range(4 * (_half + 1)):
        _q = max(_kt * P, 512 * _half)
        PIECES.append((_kt, _q, 512 * (_half + 1) - _q, _col))
        _col += 512 * (_half + 1) - _q
PCOLS = _col
NPC = len(PIECES)
SLOTS = 2 * NPC
RING = 4
MPIECES = [(qt, hh, hf, min(512, (qt + 1) * P - 512 * hf))
           for qt in range(BT) for hh in range(2) for hf in range(1 if qt < 4 else 2)]
NMP = len(MPIECES)
MAX_AT = {5: (0, 1), 7: (2, 3), 9: (4, 5), 11: (6, 7)}
MAX_AT.update({12 + i: (8 + 2 * i, 9 + 2 * i) for i in range(8)})
VALUES_AT = {8: (0, (0, 1, 2, 3)), 14: (0, (4,)), 15: (0, (5,)), 16: (0, (6,)), 17: (0, (7,)),
             20: (1, (0, 1, 2, 3))}
Q_AT = [0, 5 * D]
K_AT = [2 * D, 7 * D]
HALVES = 10 * D
TP_USES = BT + 1 + 2
SIDE_USES = NMP + BT // 2


def project_at(s):
    return s // 2 + 2 if s % 2 == 0 and s // 2 + 2 < BT else None


def pack_at(s):
    return 0 if s == 0 else (s + 1) // 2 if s % 2 == 1 and (s + 1) // 2 < BT else None


def first(n):
    return isinstance(n, int) and n == 0


def before_pack(n, t):
    return t if first(n) else TP_USES * n - 2 + t


def before_maxima(n):
    return before_pack(n, BT)


def before_context(n, g):
    return (TP_USES * n + 2 * (BT + 1) if not (isinstance(n, int) and n == NU - 1) else TP_USES * n + BT + 1) + g


def before_max(n, i):
    return i if first(n) else SIDE_USES * n - BT // 2 + i


def before_output(n, j):
    return (SIDE_USES * n + NMP + (NMP if not (isinstance(n, int) and n == NU - 1) else 0)) + j


def program(nc, ids, emb, wqkv, wo, router, gate, up, down, rope_c, rope_s, out):
    xs = nc.dram_tensor("slot_x", (SLOT_TILES * P, DM), F32).ap()
    ys = nc.dram_tensor("slot_y", (SLOT_TILES * P, DM), F32).ap()
    top = ExitStack()
    with top:
        def sbt(ctx, name, shape, dt):
            return ctx.enter_context(nc.sbuf_tensor(name, shape, dt))

        def sem(ctx, name):
            return ctx.enter_context(nc.semaphore(name))

        h = sbt(top, "h", [P, NT, DM], F32)
        ident = sbt(top, "ident", [P, P], F32)
        stats = sbt(top, "stats", [P, 2, 6], F32)
        mv = sbt(top, "mv", [P, NT, 2], F32)
        veps = sbt(top, "veps", [P, NT], F32)
        std = sbt(top, "std", [P, NT], F32)
        rstd = sbt(top, "rstd", [P, NT], F32)
        banks = [top.enter_context(nc.psum_tensor(f"bank{i}", [P, 512], F32)) for i in range(8)]

        attention(nc, sbt, sem, h, ident, (stats, mv, veps, std, rstd), banks,
                  ids, emb, wqkv, wo, rope_c, rope_s, xs)
        experts(nc, sbt, sem, h, ident, (stats, mv, veps, std, rstd), banks,
                router, gate, up, down, xs, ys, out)


def layernorm_stats(nc, dve, act_ready, act_done, stat_done, h, norm):
    stats, mv, veps, std, rstd = norm
    for t in range(NT):
        nc.vector.bn_stats(stats[:, t % 2, :], h[:, t, :]).then_inc(stat_done, 1)
        dve.wait_ge(stat_done, 2 * t + 1)
        nc.vector.bn_aggr(mv[:, t, :], stats[:, t % 2, :]).then_inc(stat_done, 1)
    dve.wait_ge(stat_done, 2 * NT)
    nc.vector.tensor_scalar(veps[:], mv[:, :, 1], EPS, None, ALU.add).then_inc(act_ready, 1)
    dve.wait_ge(act_done, 1)
    nc.vector.reciprocal(rstd[:], std[:]).then_inc(stat_done, 1)
    dve.wait_ge(stat_done, 2 * NT + 1)


def attention(nc, sbt, sem, h, ident, norm, banks, ids, emb, wqkv, wo, rope_c, rope_s, xs):
    stats, mv, veps, std, rstd = norm
    ctx = ExitStack()
    with ctx:
        def sb(name, shape, dt):
            return sbt(ctx, name, shape, dt)

        def sm(name):
            return sem(ctx, name)

        ids_sb = sb("ids_sb", [P, NT], I32)
        ident16 = sb("ident16", [P, P], F16)
        identb = sb("identb", [P, P], BF16)
        mask_q = sb("mask_q", [P, P], BF16)
        mask_k = sb("mask_k", [P, P], BF16)
        maskf = sb("maskf", [P, 2, P], F32)
        zeros = sb("zeros", [P, DM], F32)
        xn = sb("xn", [P, 4, DM], F32)
        x16 = sb("x16", [P, 4, 2, DM], F16)
        xT = sb("xT", [P, 2, KC, T], F16)
        w16 = sb("w16", [P, 2, KC, NP_, 384], F16)
        wo_sb = sb("wo_sb", [P, NP_, DM], F32)
        rc = sb("rc", [P, BT, 4, D], F32)
        rs = sb("rs", [P, BT, 4, D], F32)
        rope_a = sb("rope_a", [P, 2, 4, D], F32)
        rope_b = sb("rope_b", [P, 2, 4, D], F32)
        roped = sb("roped", [P, 2, 4, D], F32)
        halves = sb("halves", [P, 2, HALVES], F16)
        stack = sb("stack", [P, B, 4, S], F16)
        aug = sb("aug", [65, B, 4, S], F16)
        v = sb("v", [P, 2, B, BT, 2, D + 1], F16)
        probs = sb("probs", [P, 2, PCOLS], F32)
        p32 = sb("p32", [P, RING, 512], F32)
        mx = sb("mx", [P, 2, 16], F32)
        mneg = sb("mneg", [P, 2, 16], F32)
        m16 = sb("m16", [P, 16], F16)
        mT = sb("mT", [16, P], F16)
        rsum = sb("rsum", [P, 4], F32)
        cx = sb("cx", [P, BT, 2, D], F32)
        cT = sb("cT", [P, 2, 512], F32)

        p16 = [probs[:, a, :].bitcast(F16).rearrange("p (h c) -> p h c", h=2) for a in range(2)]
        w32 = probs[:, :, :].rearrange("p a c -> p (a c)")[:, 0:KC * NP_ * 384]
        w16hi = w16[:, 0].rearrange("p k u c -> p (k u c)")
        w16lo = w16[:, 1].rearrange("p k u c -> p (k u c)")
        xT_all = xT[:, :, :, :].rearrange("p a k t -> p (a k) t")

        qkv_ps = [banks[0], banks[7]]
        tp_ps = banks[1]
        tp16 = tp_ps[:, :].bitcast(F16)
        side_ps = banks[2:4]
        st_ps = banks[4:6]
        ctx_ps = banks[6]

        s_ids, s_emb, s_zero, s_fill = sm("s_ids"), sm("s_emb"), sm("s_zero"), sm("s_fill")
        s_rope_tab, s_wqkv, s_wo = sm("s_rope_tab"), sm("s_wqkv"), sm("s_wo")
        s_c, s_const = sm("s_c"), sm("s_const")
        s_whi, s_wlo = sm("s_whi"), sm("s_wlo")
        s_stat, s_var, s_std = sm("s_stat"), sm("s_var"), sm("s_std")
        s_xn, s_xhi, s_xlo = sm("s_xn"), sm("s_xhi"), sm("s_xlo")
        s_xtp, s_xT = sm("s_xtp"), sm("s_xT")
        s_setup = sm("s_setup")
        qkv_ready, rope_terms, roped_ready = sm("qkv_ready"), sm("rope_terms"), sm("roped_ready")
        hi_ready, lo_ready, twice_ready = sm("hi_ready"), sm("lo_ready"), sm("twice_ready")
        vhi_ready, qkv_free = sm("vhi_ready"), sm("qkv_free")
        pack_tp, max_tp, ctx_tp, tp_free = sm("pack_tp"), sm("max_tp"), sm("ctx_tp"), sm("tp_free")
        max_ready, y_ready, side_free = sm("max_ready"), sm("y_ready"), sm("side_free")
        mneg_ready, m16_ready, mrow_ready = sm("mneg_ready"), sm("m16_ready"), sm("mrow_ready")
        st_ready, st_free, plo_done = sm("st_ready"), sm("st_free"), sm("plo_done")
        pv_ready, rsum_ready, ctx_free = sm("pv_ready"), sm("rsum_ready"), sm("ctx_free")

        block = ctx.enter_context(nc.Block())

        @block.sync
        def _(sp):
            sp.dma_start(ids_sb[:], ids).then_inc(s_ids, 16)
            sp.dma_start(w32, wqkv).then_inc(s_wqkv, 16)
            sp.dma_start(rc[:, :, :, :].rearrange("p t a d -> p (t a d)"), rope_c).then_inc(s_rope_tab, 16)
            sp.dma_start(rs[:, :, :, :].rearrange("p t a d -> p (t a d)"), rope_s).then_inc(s_rope_tab, 16)
            sp.dma_start(wo_sb[:, :, :].rearrange("p u n -> p (u n)"), wo).then_inc(s_wo, 16)
            sp.wait_ge(s_zero, 1)
            sp.dma_start(xs.rearrange("(p r) d -> p r d", r=SLOT_TILES),
                         zeros[:, :].unsqueeze(1).to_broadcast([P, SLOT_TILES, DM])).then_inc(s_fill, 16)

            def max_row(n, b):
                sp.wait_ge(tp_free, before_maxima(n) + 1)
                for hh in range(2):
                    sp.dma_start(aug[64:65, b, hh, :],
                                 mT[8 * hh:8 * hh + 8, :]).then_inc(mrow_ready, 16)

            max_row(0, 0)
            with sp.Fori(0, NP_ - 1) as p:
                max_row(2 * p + 1, 1)
                max_row(2 * p + 2, 0)
            max_row(NU - 1, 1)
            sp.wait_ge(s_fill, 16)

        @block.gpsimd
        def _(pool):
            nc.gpsimd.memset(zeros[:], 0.0).then_inc(s_zero, 1)
            pool.wait_ge(s_ids, 16)
            for t in range(NT):
                nc.gpsimd.indirect_dma_start(
                    out=h[:, t, :], out_offset=None, in_=emb,
                    in_offset=bass.IndirectOffsetOnAxis(ap=ids_sb[:, t:t + 1], axis=0)).then_inc(s_emb, 16)
            nc.gpsimd.memset(ident[:], 0.0).then_inc(s_c, 1)
            nc.gpsimd.memset(maskf[:], 0.0).then_inc(s_c, 1)
            pool.wait_ge(s_c, 2)
            nc.gpsimd.affine_select(out=ident[:], in_=ident[:], compare_op=ALU.not_equal, fill=1.0, base=0,
                                    pattern=[[-1, P]], channel_multiplier=1).then_inc(s_c, 1)
            nc.gpsimd.affine_select(out=maskf[:, 0, :], in_=maskf[:, 0, :], compare_op=ALU.is_ge, fill=NEG, base=0,
                                    pattern=[[-1, P]], channel_multiplier=1).then_inc(s_c, 1)
            nc.gpsimd.affine_select(out=maskf[:, 1, :], in_=maskf[:, 1, :], compare_op=ALU.is_ge, fill=NEG, base=0,
                                    pattern=[[1, P]], channel_multiplier=-1).then_inc(s_c, 1)
            pool.wait_ge(s_c, 5)
            nc.gpsimd.tensor_copy(ident16[:], ident[:]).then_inc(s_const, 1)
            nc.gpsimd.tensor_copy(identb[:], ident[:]).then_inc(s_const, 1)
            nc.gpsimd.tensor_copy(mask_q[:], maskf[:, 0, :]).then_inc(s_const, 1)
            nc.gpsimd.tensor_copy(mask_k[:], maskf[:, 1, :]).then_inc(s_const, 1)
            pool.sem_inc(s_xlo, 4)
            with pool.Fori(0, NT // 4) as g:
                for j in range(4):
                    pool.wait_ge(s_xhi, 4 * g + j + 1)
                    nc.gpsimd.tensor_tensor(x16[:, j, 1, :], xn[:, j, :], x16[:, j, 0, :],
                                            ALU.subtract).then_inc(s_xlo, 1)

            def low_halves(n, s):
                kt, q, w, c = PIECES[s % NPC]
                pool.wait_ge(st_free, 2 + SLOTS * n + s + 1)
                nc.gpsimd.tensor_tensor(p16[1][:, s // NPC, c:c + w], p32[:, s % RING, 0:w],
                                        p16[0][:, s // NPC, c:c + w], ALU.subtract).then_inc(plo_done, 1)

            pool.sem_inc(plo_done, RING)
            with pool.Fori(0, NU) as n:
                for s in range(SLOTS):
                    low_halves(n, s)

        @block.scalar
        def _(act):
            act.wait_ge(s_wqkv, 16)
            nc.scalar.activation(w16hi, w32, ACT.Copy, scale=W_SCALE).then_inc(s_whi, 1)
            act.wait_ge(s_var, 1)
            nc.scalar.activation(std[:], veps[:], ACT.Sqrt).then_inc(s_std, 1)
            act.sem_inc(s_xT, 2)
            with act.Fori(0, NT // 4) as g:
                for j in range(4):
                    act.wait_ge(s_xn, 4 * g + j + 1)
                    nc.scalar.activation(x16[:, j, 0, :], xn[:, j, :], ACT.Copy).then_inc(s_xhi, 1)
                for j in range(4):
                    act.wait_ge(s_xtp, 4 * g + j + 1)
                    nc.scalar.activation(xT_all[:, :, bass.ds(512 * g + P * j, P)],
                                         banks[j % 2][:, :].bitcast(F16)[:, 0:512].rearrange("p (a t) -> p a t", a=4),
                                         ACT.Copy).then_inc(s_xT, 1)

            def value_high(n, b, t):
                act.wait_ge(rope_terms, 2 * (BT * n + t) + 2)
                nc.scalar.activation(v[:, 0, b, t, :, 0:D],
                                     qkv_ps[t % 2][:, 256:384].rearrange("p (h d) -> p h d", h=2),
                                     ACT.Copy).then_inc(vhi_ready, 1)

            def keys_twice(n, t):
                act.wait_ge(hi_ready, BT * n + t + 1)
                k = halves[:, t % 2].rearrange("p (a c) -> p a c", a=2)
                nc.scalar.activation(k[:, :, K_AT[0] + D:K_AT[0] + 2 * D], k[:, :, K_AT[0]:K_AT[0] + D],
                                     ACT.Copy).then_inc(twice_ready, 1)

            def stacks(n, b, t):
                act.wait_ge(pack_tp, BT * n + t + 1)
                nc.scalar.activation(stack[:, b, :, t * P:(t + 1) * P],
                                     tp16[:, 0:512].rearrange("p (a t) -> p a t", a=4), ACT.Copy)
                nc.scalar.activation(aug[0:64, b, :, t * P:(t + 1) * P],
                                     tp16[0:64, 256:768].rearrange("p (a t) -> p a t", a=4),
                                     ACT.Copy).then_inc(tp_free, 1)

            def exps(n, s):
                kt, q, w, c = PIECES[s % NPC]
                act.wait_ge(st_ready, SLOTS * n + s + 1)
                act.wait_ge(plo_done, SLOTS * n + s + 1)
                nc.scalar.activation(p32[:, s % RING, 0:w], st_ps[s % 2][:, 0:w], ACT.Exp)
                nc.scalar.activation(p16[0][:, s // NPC, c:c + w], st_ps[s % 2][:, 0:w],
                                     ACT.Exp).then_inc(st_free, 1)

            def maxima(n):
                act.wait_ge(max_tp, n + 1)
                nc.scalar.activation(mT[:], tp16[0:16, 0:P], ACT.Copy).then_inc(tp_free, 1)

            def context(n, g):
                act.wait_ge(ctx_tp, 2 * n + g + 1)
                nc.scalar.activation(cT[:, g, :], tp_ps[:, :], ACT.Copy).then_inc(tp_free, 1)

            def unit(n, b, nxt, nxt2):
                for s in range(SLOTS):
                    exps(n, s)
                    if nxt:
                        late = project_at(s - 1)
                        if late is not None:
                            value_high(n + 1, 1 - b, late)
                        if pack_at(s) is not None:
                            stacks(n + 1, 1 - b, pack_at(s))
                        if late is not None:
                            keys_twice(n + 1, late)
                if nxt:
                    maxima(n + 1)
                context(n, 0)
                if nxt2:
                    value_high(n + 2, b, 0)
                    keys_twice(n + 2, 0)
                context(n, 1)
                if nxt2:
                    value_high(n + 2, b, 1)
                    keys_twice(n + 2, 1)

            act.sem_inc(st_free, 2)
            for t in range(BT + 1):
                if t < BT:
                    value_high(0, 0, t)
                    keys_twice(0, t)
                if t > 0:
                    stacks(0, 0, t - 1)
            for t in range(2):
                value_high(1, 1, t)
                keys_twice(1, t)
            maxima(0)
            with act.Fori(0, NP_ - 1) as p:
                unit(2 * p, 0, True, True)
                unit(2 * p + 1, 1, True, True)
            unit(NU - 2, 0, True, False)
            unit(NU - 1, 1, False, False)

        @block.tensor
        def _(pe):
            pe.wait_ge(s_const, 4)
            with pe.Fori(0, NT // 4) as g:
                for j in range(4):
                    pe.wait_ge(s_xlo, 4 + 4 * g + j + 1)
                    pe.wait_ge(s_xT, 4 * g + j + 1)
                    for a in range(4):
                        mm = nc.tensor.transpose(banks[j % 2][:, :].bitcast(F16)[:, a * P:(a + 1) * P],
                                                 x16[:, j, a // 2, (a % 2) * P:(a % 2 + 1) * P], ident16[:])
                    mm.then_inc(s_xtp, 1)
            pe.wait_ge(s_xT, NT + 2)
            pe.wait_ge(s_wlo, 1)

            def project(n, p, b, t):
                i = BT * n + t
                if not (isinstance(i, int) and i < 2):
                    pe.wait_ge(qkv_free, i - 1)
                tok = S * b + P * t
                for kc in range(KC):
                    for a, c in ((0, 0), (0, 1), (1, 0)):
                        mm = nc.tensor.matmul(qkv_ps[t % 2][:, 0:384], xT[:, a, kc, tok:tok + P],
                                              w16[:, c, kc, bass.ds(p, 1), :].rearrange("p o c -> p (o c)"),
                                              start=(kc == 0 and a == 0 and c == 0), stop=(kc == KC - 1 and a == 1))
                mm.then_inc(qkv_ready, 1)

            def pack(n, t):
                i = t % 2
                pe.wait_ge(lo_ready, BT * n + t + 1)
                pe.wait_ge(twice_ready, BT * n + t + 1)
                w = before_pack(n, t)
                if not (isinstance(w, int) and w == 0):
                    pe.wait_ge(tp_free, w)
                for hh in range(2):
                    k, q = K_AT[hh], Q_AT[hh]
                    nc.tensor.transpose(tp16[:, hh * P:(hh + 1) * P], halves[:, i, k:k + 2 * D], ident16[:])
                    nc.tensor.transpose(tp16[:, (2 + hh) * P:(3 + hh) * P], halves[:, i, q:q + 2 * D], ident16[:])
                    mm = nc.tensor.transpose(tp16[0:D, (4 + hh) * P:(5 + hh) * P],
                                             halves[:, i, k + 2 * D:k + 3 * D], ident16[:])
                mm.then_inc(pack_tp, 1)

            def max_piece(n, b, i):
                qt, hh, hf, w = MPIECES[i]
                u = before_max(n, i)
                if not (isinstance(u, int) and u < 2):
                    pe.wait_ge(side_free, u - 1)
                pe.wait_ge(tp_free, before_pack(n, qt) + 1)
                diag = qt // 4 == hf
                ps = side_ps[i % 2]
                mm = nc.tensor.matmul(ps[:, 0:w], stack[:, b, 2 + hh, qt * P:(qt + 1) * P],
                                      stack[:, b, hh, 512 * hf:512 * hf + w], start=True, stop=not diag)
                if diag:
                    mm = nc.tensor.matmul(ps[:, w - P:w], identb[:], mask_q[:], start=False, stop=True)
                mm.then_inc(max_ready, 1)

            def max_rows(n):
                pe.wait_ge(m16_ready, n + 1)
                pe.wait_ge(tp_free, before_maxima(n))
                nc.tensor.transpose(tp16[0:16, 0:P], m16[:], ident16[:]).then_inc(max_tp, 1)

            def scores(n, b, s):
                kt, q, w, c = PIECES[s % NPC]
                hh = s // NPC
                pe.wait_ge(st_free, SLOTS * n + s + 1)
                ps = st_ps[s % 2]
                nc.tensor.matmul(ps[:, 0:w], stack[:, b, hh, kt * P:(kt + 1) * P], stack[:, b, 2 + hh, q:q + w],
                                 start=True, stop=False)
                mm = nc.tensor.matmul(ps[:, 0:w], aug[0:65, b, 2 + hh, kt * P:(kt + 1) * P],
                                      aug[0:65, b, hh, q:q + w], start=False, stop=(q != kt * P))
                if q == kt * P:
                    mm = nc.tensor.matmul(ps[:, 0:P], identb[:], mask_k[:], start=False, stop=True)
                mm.then_inc(st_ready, 1)

            def values(n, b, hh, tiles):
                half = tiles[0] // 4
                if tiles[0] % 4 == 0:
                    pe.wait_ge(qkv_free, BT * (n + 1))
                    last = NPC * hh + (4 if half == 0 else NPC)
                    pe.wait_ge(plo_done, RING + SLOTS * n + last)
                    pe.wait_ge(ctx_free, 4 * n + 2 * hh + half + 1)
                for qt in tiles:
                    acc = ctx_ps[:, (qt % 4) * 65:(qt % 4) * 65 + 65]
                    for kt in range(qt + 1):
                        c = [c + P * qt - q for k, q, w, c in PIECES if k == kt and q <= P * qt < q + w][0]
                        for a, d in ((0, 0), (0, 1), (1, 0)):
                            mm = nc.tensor.matmul(acc, p16[a][:, hh, c:c + P], v[:, d, b, kt, hh, :],
                                                  start=(kt == 0 and a == 0 and d == 0), stop=(kt == qt and a == 1))
                if tiles[-1] % 4 == 3:
                    mm.then_inc(pv_ready, 1)

            def context(n, g):
                pe.wait_ge(ctx_free, 1 + 4 * n + 3 + g)
                pe.wait_ge(tp_free, before_context(n, g))
                for i in range(4):
                    mm = nc.tensor.transpose(tp_ps[:, i * P:(i + 1) * P],
                                             cx[:, 4 * g + i].rearrange("p h d -> p (h d)"), ident[:])
                mm.then_inc(ctx_tp, 1)

            def output(n, p, j):
                if j % 2 == 0:
                    pe.wait_ge(tp_free, before_context(n, j // 2) + 1)
                pe.wait_ge(side_free, before_output(n, j) - 1)
                for i in range(2):
                    t = 2 * j + i
                    mm = nc.tensor.matmul(side_ps[j % 2][:, i * DM:(i + 1) * DM],
                                          cT[:, t // 4, (t % 4) * P:(t % 4 + 1) * P],
                                          wo_sb[:, bass.ds(p, 1), :].rearrange("p o c -> p (o c)"),
                                          start=True, stop=True)
                mm.then_inc(y_ready, 1)

            def unit(n, p, b, nxt, nxt2):
                pe.wait_ge(mrow_ready, 32 * (n + 1))
                for s in range(SLOTS):
                    scores(n, b, s)
                    if nxt:
                        if project_at(s) is not None:
                            project(n + 1, p + b, 1 - b, project_at(s))
                        if pack_at(s) is not None:
                            pack(n + 1, pack_at(s))
                    if s in VALUES_AT:
                        values(n, b, *VALUES_AT[s])
                    if nxt:
                        for i in MAX_AT.get(s, ()):
                            max_piece(n + 1, 1 - b, i)
                if nxt:
                    max_rows(n + 1)
                context(n, 0)
                output(n, p, 0)
                output(n, p, 1)
                values(n, b, 1, (4, 5, 6, 7))
                if nxt2:
                    project(n + 2, p + 1, b, 0)
                context(n, 1)
                if nxt2:
                    project(n + 2, p + 1, b, 1)
                output(n, p, 2)
                output(n, p, 3)

            for t in range(BT + 2):
                if t < BT:
                    project(0, 0, 0, t)
                else:
                    project(1, 0, 1, t - BT)
                if 0 < t <= BT:
                    pack(0, t - 1)
                for i in range(NMP):
                    if MPIECES[i][0] == t - 2:
                        max_piece(0, 0, i)
            max_rows(0)
            pe.wait_ge(s_setup, 4)
            pe.wait_ge(s_wo, 16)
            with pe.Fori(0, NP_ - 1) as p:
                unit(2 * p, p, 0, True, True)
                unit(2 * p + 1, p, 1, True, True)
            unit(NU - 2, NP_ - 1, 0, True, False)
            unit(NU - 1, NP_ - 1, 1, False, False)

        @block.vector
        def _(dve):
            nc.vector.memset(aug[64:65, :, 2:4, :], M_SCALE).then_inc(s_setup, 1)
            nc.vector.memset(v[:, 0, :, :, :, D:D + 1], W_SCALE).then_inc(s_setup, 1)
            nc.vector.memset(v[:, 1, :, :, :, D:D + 1], 0.0).then_inc(s_setup, 1)
            nc.vector.memset(mx[:, 1, :], -3.0e38).then_inc(s_setup, 1)
            dve.wait_ge(s_setup, 4)
            dve.wait_ge(s_emb, 16 * NT)
            layernorm_stats(nc, dve, s_var, s_std, s_stat, h, norm)
            with dve.Fori(0, NT // 4) as g:
                for j in range(4):
                    t = 4 * g + j
                    dve.wait_ge(s_xlo, t + 1)
                    nc.vector.tensor_scalar(xn[:, j, :], h[:, bass.ds(t, 1), :].rearrange("p o c -> p (o c)"),
                                            mv[:, bass.ds(t, 1), 0], rstd[:, bass.ds(t, 1)],
                                            ALU.subtract, ALU.mult).then_inc(s_xn, 1)
            dve.wait_ge(s_whi, 1)
            nc.vector.scalar_tensor_tensor(w16lo, w32, W_SCALE, w16hi, ALU.mult, ALU.subtract).then_inc(s_wlo, 1)
            dve.wait_ge(s_rope_tab, 32)

            def rotate(n, t):
                i = t % 2
                g = BT * n + t
                ps = qkv_ps[i]
                dve.wait_ge(qkv_ready, g + 1)
                qk = ps[:, 0:256].rearrange("p (a d) -> p a d", a=4)
                nc.vector.tensor_tensor(rope_a[:, i], qk, rc[:, t], ALU.mult).then_inc(rope_terms, 1)
                swapped = bass.AP(ps, D // 2, [[512, P], [D, 4], [-(D // 2), 2], [1, D // 2]])
                nc.vector.tensor_tensor(rope_b[:, i].rearrange("p a (s d) -> p a s d", s=2), swapped,
                                        rs[:, t].rearrange("p a (s d) -> p a s d", s=2),
                                        ALU.mult).then_inc(rope_terms, 1)
                dve.wait_ge(rope_terms, 2 * g + 2)
                nc.vector.tensor_tensor(roped[:, i], rope_a[:, i], rope_b[:, i], ALU.add).then_inc(roped_ready, 1)
                r = roped[:, i].rearrange("p (a h) d -> p a h d", a=2)
                hi = bass.AP(halves, HALVES * i, [[2 * HALVES, P], [K_AT[0], 2], [5 * D, 2], [1, D]])
                lo = bass.AP(halves, HALVES * i + D, [[2 * HALVES, P], [K_AT[0] + D, 2], [5 * D, 2], [1, D]])
                dve.wait_ge(roped_ready, g + 1)
                if not (isinstance(g, int) and g < 2):
                    dve.wait_ge(pack_tp, g - 1)
                nc.vector.tensor_copy(hi, r).then_inc(hi_ready, 1)
                dve.wait_ge(hi_ready, g + 1)
                nc.vector.tensor_tensor(lo, r, hi, ALU.subtract).then_inc(lo_ready, 1)

            def value_low(n, b, t):
                dve.wait_ge(vhi_ready, BT * n + t + 1)
                nc.vector.tensor_tensor(v[:, 1, b, t, :, 0:D],
                                        qkv_ps[t % 2][:, 256:384].rearrange("p (h d) -> p h d", h=2),
                                        v[:, 0, b, t, :, 0:D], ALU.subtract).then_inc(qkv_free, 1)

            def maximum(n, i):
                qt, hh, hf, w = MPIECES[i]
                dve.wait_ge(max_ready, NMP * n + i + 1)
                nc.vector.reduce_max(mx[:, hf, 8 * hh + qt:8 * hh + qt + 1], side_ps[i % 2][:, 0:w],
                                     AX.X).then_inc(side_free, 1)

            def negate(n):
                dve.wait_ge(side_free, before_max(n, NMP))
                nc.vector.tensor_scalar(mneg[:], mx[:], -1.0 / M_SCALE, None, ALU.mult).then_inc(mneg_ready, 1)
                dve.wait_ge(mneg_ready, n + 1)
                nc.vector.tensor_tensor(m16[:], mneg[:, 0, :], mneg[:, 1, :], ALU.min).then_inc(m16_ready, 1)

            def normalize(n, hh, g):
                i = 4 * n + 2 * hh + g
                acc = ctx_ps[:, 0:260].rearrange("p (q d) -> p q d", q=4)
                dve.wait_ge(pv_ready, i + 1)
                nc.vector.reciprocal(rsum[:], acc[:, :, D]).then_inc(rsum_ready, 1)
                dve.wait_ge(rsum_ready, i + 1)
                nc.vector.tensor_tensor(cx[:, 4 * g:4 * g + 4, hh, :], acc[:, :, 0:D],
                                        rsum[:, :].unsqueeze(2).to_broadcast([P, 4, D]),
                                        ALU.mult).then_inc(ctx_free, 1)

            def residual(n, b, j):
                dve.wait_ge(y_ready, 4 * n + j + 1)
                rows = h[:, BT * b + 2 * j:BT * b + 2 * j + 2, :]
                nc.vector.tensor_tensor(rows, side_ps[j % 2][:, :].rearrange("p (t c) -> p t c", t=2), rows,
                                        ALU.add).then_inc(side_free, 1)

            def unit(n, b, nxt, nxt2):
                for s in range(SLOTS):
                    if nxt:
                        if project_at(s) is not None:
                            rotate(n + 1, project_at(s))
                        if project_at(s - 1) is not None:
                            value_low(n + 1, 1 - b, project_at(s - 1))
                    if s - 1 in VALUES_AT and VALUES_AT[s - 1][1][-1] % 4 == 3:
                        normalize(n, VALUES_AT[s - 1][0], VALUES_AT[s - 1][1][-1] // 4)
                    if nxt:
                        for i in MAX_AT.get(s, ()):
                            maximum(n + 1, i)
                        if s == max(MAX_AT):
                            negate(n + 1)
                residual(n, b, 0)
                residual(n, b, 1)
                normalize(n, 1, 1)
                if nxt2:
                    rotate(n + 2, 0)
                    value_low(n + 2, b, 0)
                    rotate(n + 2, 1)
                residual(n, b, 2)
                if nxt2:
                    value_low(n + 2, b, 1)
                residual(n, b, 3)

            dve.sem_inc(ctx_free, 1)
            for t in range(BT + 2):
                n = t // BT
                rotate(n, t % BT)
                value_low(n, n, t % BT)
                for i in range(NMP):
                    if MPIECES[i][0] == t - 2:
                        maximum(0, i)
            negate(0)
            with dve.Fori(0, NP_ - 1) as p:
                unit(2 * p, 0, True, True)
                unit(2 * p + 1, 1, True, True)
            unit(NU - 2, 0, True, False)
            unit(NU - 1, 1, False, False)


def experts(nc, sbt, sem, h, ident, norm, banks, router, gate, up, down, xs, ys, out):
    stats, mv, veps, std, rstd = norm
    ctx = ExitStack()
    with ctx:
        pos = sbt(ctx, "pos", [P, TOPK, NT], I32)
        gates = sbt(ctx, "gates", [P, NT, 8], F32)
        tile_expert = sbt(ctx, "tile_expert", [1, SLOT_TILES], I32)
        gate_sb = sbt(ctx, "gate_sb", [P, E, KC, FF], F32)
        up_sb = sbt(ctx, "up_sb", [P, E, KC, FF], F32)
        down_sb = sbt(ctx, "down_sb", [P, E, FC, DM], F32)
        weights_in = sem(ctx, "weights_in")
        tail_zero = sem(ctx, "tail_zero")
        with ExitStack() as c:
            route(nc, c, sbt, sem, h, ident, norm, banks, router, gate, up, down, xs,
                  pos, gates, tile_expert, gate_sb, up_sb, down_sb, weights_in, tail_zero)
        with ExitStack() as c:
            feed_forward(nc, c, sbt, sem, ident, banks, xs, ys, tile_expert, gate_sb, up_sb, down_sb,
                         weights_in, tail_zero)
        with ExitStack() as c:
            combine(nc, c, sbt, sem, h, ys, pos, gates, out)


def route(nc, ctx, sbt, sem, h, ident, norm, banks, router, gate, up, down, xs,
          pos, gates, tile_expert, gate_sb, up_sb, down_sb, weights_in, tail_zero):
    stats, mv, veps, std, rstd = norm

    def sb(name, shape, dt):
        return sbt(ctx, name, shape, dt)

    def sm(name):
        return sem(ctx, name)

    xn = sb("xn2", [P, NT, DM], F32)
    xT = sb("xT2", [P, 2, KC, P], F32)
    router_sb = sb("router_sb", [P, KC, E], F32)
    logits = sb("logits", [P, NT, E], F32)
    shifted = sb("shifted", [P, NT, E], F32)
    expd = sb("expd", [P, NT, E], F32)
    rmax = sb("rmax", [P, NT], F32)
    total = sb("total", [P, NT], F32)
    inv = sb("inv", [P, NT], F32)
    pr = sb("pr", [P, NT, E], F32)
    idx = sb("idx", [P, NT, 8], U32)
    idxf = sb("idxf", [P, NT, 2], F32)
    iota_e = sb("iota_e", [P, E], F32)
    iota_t = sb("iota_t", [1, SLOT_TILES], F32)
    before = sb("before", [P, P], F32)
    ones = sb("ones", [P, P], F32)
    hot = sb("hot", [P, TOPK, NT, E], F32)
    chosen = sb("chosen", [P, NT, E], F32)
    cum = sb("cum", [P, 2, NT, E], F32)
    rank = sb("rank", [P, NT, E], F32)
    cnt_i = sb("cnt_i", [P, E], I32)
    cnt_s = sb("cnt_s", [P, E], I32)
    tiles = sb("tiles", [P, E], F32)
    ecum = sb("ecum", [P, 2, E], F32)
    base = sb("base", [P, E], F32)
    picked = sb("picked", [P, TOPK, NT, E], F32)
    posf = sb("posf", [P, TOPK, NT], F32)
    past = sb("past", [1, SLOT_TILES, E], F32)
    texp = sb("texp", [1, SLOT_TILES], F32)

    c_made, c_sel = sm("c_made"), sm("c_sel")
    r_in = sm("r_in")
    stat, var, root = sm("stat"), sm("var"), sm("root")
    xn_ready, xtp, xt_ready, lg_ready = sm("xn_ready2"), sm("xtp2"), sm("xt_ready2"), sm("lg_ready2")
    sh_ready, ex_ready = sm("sh_ready"), sm("ex_ready")
    chosen_ready, ranks_ready, step_done, pos_ready = sm("chosen_ready"), sm("ranks_ready"), sm("step_done"), sm("pos_ready")
    scattered = sm("scattered")

    block = ctx.enter_context(nc.Block())

    @block.sync
    def _(sp):
        sp.dma_start(router_sb[:, :, :].rearrange("p k e -> p (k e)"), router).then_inc(r_in, 16)
        for e in range(E):
            sp.dma_start(gate_sb[:, e].rearrange("p k f -> p (k f)"), gate[e]).then_inc(weights_in, 16)
            sp.dma_start(up_sb[:, e].rearrange("p k f -> p (k f)"), up[e]).then_inc(weights_in, 16)
            sp.dma_start(down_sb[:, e, 0:FF // P, :],
                         down[e, 0:FF // P * P, :].rearrange("(c p) d -> p c d", p=P)).then_inc(weights_in, 16)
            sp.dma_start(down_sb[0:FF % P, e, FC - 1, :], down[e, FF // P * P:FF, :]).then_inc(weights_in, 16)

    @block.gpsimd
    def _(pool):
        nc.gpsimd.memset(down_sb[FF % P:P, :, FC - 1, :], 0.0).then_inc(tail_zero, 1)
        pool.wait_ge(tail_zero, 1)
        nc.gpsimd.iota(iota_e[:], pattern=[[1, E]], base=0, channel_multiplier=0,
                       allow_small_or_imprecise_dtypes=True).then_inc(c_made, 1)
        nc.gpsimd.iota(iota_t[:], pattern=[[1, SLOT_TILES]], base=0, channel_multiplier=0,
                       allow_small_or_imprecise_dtypes=True).then_inc(c_made, 1)
        nc.gpsimd.memset(ones[:], 1.0).then_inc(c_sel, 1)
        pool.wait_ge(c_sel, 1)
        nc.gpsimd.affine_select(out=before[:], in_=ones[:], compare_op=ALU.is_gt, fill=0.0, base=0,
                                pattern=[[1, P]], channel_multiplier=-1).then_inc(c_made, 1)
        pool.wait_ge(pos_ready, 1)
        for k in range(TOPK):
            for t in range(NT):
                nc.gpsimd.indirect_dma_start(
                    out=xs, out_offset=bass.IndirectOffsetOnAxis(ap=pos[:, k, t:t + 1], axis=0),
                    in_=xn[:, t, :], in_offset=None).then_inc(scattered, 16)
        pool.wait_ge(scattered, 16 * TOPK * NT)

    @block.scalar
    def _(act):
        act.wait_ge(var, 1)
        nc.scalar.activation(std[:], veps[:], ACT.Sqrt).then_inc(root, 1)
        for t in range(NT):
            act.wait_ge(xtp, t + 1)
            nc.scalar.activation(xT[:, t % 2].rearrange("p k t -> p (k t)"), banks[t % 2][:, 0:KC * P],
                                 ACT.Copy).then_inc(xt_ready, 1)
        act.wait_ge(sh_ready, 1)
        nc.scalar.activation(expd[:], shifted[:], ACT.Exp).then_inc(ex_ready, 1)

    @block.tensor
    def _(pe):
        pe.wait_ge(r_in, 16)

        def logit(t):
            pe.wait_ge(xt_ready, t + 1)
            for kc in range(KC):
                mm = nc.tensor.matmul(banks[2][:, t * E:(t + 1) * E], xT[:, t % 2, kc, :], router_sb[:, kc, :],
                                      start=(kc == 0), stop=(kc == KC - 1))
            mm.then_inc(lg_ready, 1)

        for t in range(NT):
            pe.wait_ge(xn_ready, t + 1)
            if t >= 2:
                pe.wait_ge(xt_ready, t - 1)
            for kc in range(KC):
                mm = nc.tensor.transpose(banks[t % 2][:, kc * P:(kc + 1) * P], xn[:, t, kc * P:(kc + 1) * P], ident[:])
            mm.then_inc(xtp, 1)
            if t >= 1:
                logit(t - 1)
        logit(NT - 1)
        pe.wait_ge(chosen_ready, 1)
        pe.wait_ge(c_made, 3)
        flat = chosen[:, :, :].rearrange("p t e -> p (t e)")
        nc.tensor.matmul(banks[3][:, 0:NT * E], before[:], flat, start=True, stop=True)
        nc.tensor.matmul(banks[4][:, 0:NT * E], ones[:], flat, start=True, stop=True).then_inc(ranks_ready, 1)

    @block.vector
    def _(dve):
        done = [0]

        def step(ins):
            done[0] += 1
            ins.then_inc(step_done, 1)
            dve.wait_ge(step_done, done[0])

        layernorm_stats(nc, dve, var, root, stat, h, norm)
        for t in range(NT):
            nc.vector.tensor_scalar(xn[:, t, :], h[:, t, :], mv[:, t, 0:1], rstd[:, t:t + 1],
                                    ALU.subtract, ALU.mult).then_inc(xn_ready, 1)
        dve.wait_ge(lg_ready, NT)
        step(nc.vector.tensor_copy(logits[:, :, :].rearrange("p t e -> p (t e)"), banks[2][:, 0:NT * E]))
        step(nc.vector.reduce_max(rmax[:], logits[:], AX.X))
        nc.vector.tensor_tensor(shifted[:], logits[:], rmax[:, :].unsqueeze(2).to_broadcast([P, NT, E]),
                                ALU.subtract).then_inc(sh_ready, 1)
        dve.wait_ge(ex_ready, 1)
        step(nc.vector.reduce_sum(total[:], expd[:], AX.X))
        step(nc.vector.reciprocal(inv[:], total[:]))
        step(nc.vector.tensor_tensor(pr[:], expd[:], inv[:, :].unsqueeze(2).to_broadcast([P, NT, E]), ALU.mult))
        for t in range(NT):
            last = nc.vector.max(gates[:, t, :], pr[:, t, :])
        step(last)
        for t in range(NT):
            last = nc.vector.max_index(idx[:, t, :], gates[:, t, :], pr[:, t, :])
        step(last)
        step(nc.vector.tensor_copy(idxf[:], idx[:, :, 0:2]))
        dve.wait_ge(c_made, 3)
        for k in range(TOPK):
            last = nc.vector.tensor_tensor(hot[:, k], iota_e[:, :].unsqueeze(1).to_broadcast([P, NT, E]),
                                           idxf[:, :, k].unsqueeze(2).to_broadcast([P, NT, E]), ALU.is_equal)
        step(last)
        nc.vector.tensor_tensor(chosen[:], hot[:, 0], hot[:, 1], ALU.add).then_inc(chosen_ready, 1)
        dve.wait_ge(ranks_ready, 1)
        tile_cnt = banks[4][:, 0:NT * E].rearrange("p (t e) -> p t e", e=E)
        step(nc.vector.tensor_copy(cum[:, 0], tile_cnt))
        a, d = 0, 1
        while d < NT:
            nc.vector.tensor_copy(cum[:, 1 - a, 0:d, :], cum[:, a, 0:d, :])
            step(nc.vector.tensor_tensor(cum[:, 1 - a, d:NT, :], cum[:, a, d:NT, :], cum[:, a, 0:NT - d, :], ALU.add))
            a, d = 1 - a, 2 * d
        step(nc.vector.tensor_scalar(cnt_i[:], cum[:, a, NT - 1, :], float(P - 1), None, ALU.add))
        step(nc.vector.tensor_scalar(cnt_s[:], cnt_i[:], 7, None, ALU.arith_shift_right))
        step(nc.vector.tensor_copy(tiles[:], cnt_s[:]))
        step(nc.vector.tensor_copy(ecum[:, 0], tiles[:]))
        ea, d = 0, 1
        while d < E:
            nc.vector.tensor_copy(ecum[:, 1 - ea, 0:d], ecum[:, ea, 0:d])
            step(nc.vector.tensor_tensor(ecum[:, 1 - ea, d:E], ecum[:, ea, d:E], ecum[:, ea, 0:E - d], ALU.add))
            ea, d = 1 - ea, 2 * d
        step(nc.vector.tensor_tensor(base[:], ecum[:, ea], tiles[:], ALU.subtract))
        step(nc.vector.tensor_tensor(rank[:], cum[:, a], tile_cnt, ALU.subtract))
        step(nc.vector.tensor_tensor(rank[:], banks[3][:, 0:NT * E].rearrange("p (t e) -> p t e", e=E), rank[:], ALU.add))
        step(nc.vector.tensor_scalar(base[:], base[:], float(P), None, ALU.mult))
        step(nc.vector.tensor_tensor(rank[:], rank[:], base[:, :].unsqueeze(1).to_broadcast([P, NT, E]), ALU.add))
        for k in range(TOPK):
            last = nc.vector.tensor_tensor(picked[:, k], hot[:, k], rank[:], ALU.mult)
        step(last)
        step(nc.vector.reduce_sum(posf[:], picked[:], AX.X))
        nc.vector.tensor_copy(pos[:], posf[:]).then_inc(pos_ready, 1)
        step(nc.vector.tensor_tensor(past[:], iota_t[:, :].unsqueeze(2).to_broadcast([1, SLOT_TILES, E]),
                                     ecum[0:1, ea].unsqueeze(1).to_broadcast([1, SLOT_TILES, E]), ALU.is_ge))
        step(nc.vector.reduce_sum(texp[:], past[:], AX.X))
        step(nc.vector.tensor_scalar(tile_expert[:], texp[:], float(E - 1), None, ALU.min))


def feed_forward(nc, ctx, sbt, sem, ident, banks, xs, ys, tile_expert, gate_sb, up_sb, down_sb,
                 weights_in, tail_zero):
    def sb(name, shape, dt):
        return sbt(ctx, name, shape, dt)

    def sm(name):
        return sem(ctx, name)

    x_in = sb("x_in", [P, 2, DM], F32)
    xT = sb("xT3", [P, 2, KC, P], F32)
    sg = sb("sg", [P, FF], F32)
    hh = sb("hh", [P, FC * P], F32)
    hT = sb("hT", [P, FC, P], F32)
    y_sb = sb("y_sb", [P, 2, DM], F32)

    x_loaded = [sm("x_loaded0"), sm("x_loaded1")]
    y_stored = [sm("y_stored0"), sm("y_stored1")]
    pad_zero, xt_tp, xt_ready = sm("pad_zero"), sm("xt_tp"), sm("xt_ready")
    g_ready, u_ready, sg_ready, hh_ready = sm("g_ready"), sm("u_ready"), sm("sg_ready"), sm("hh_ready")
    ht_tp, ht_ready, y_ready, y_free = sm("ht_tp"), sm("ht_ready"), sm("y_ready3"), sm("y_free3")

    xt_ps = banks[0]
    y_ps = banks[1]
    ht_ps = banks[2:4]
    g_ps = banks[4:6]
    u_ps = banks[6:8]
    n_loops = (SLOT_TILES - 1) // 2
    assert SLOT_TILES == 2 * n_loops + 1

    block = ctx.enter_context(nc.Block())

    @block.sync
    def _(sp):
        def load(j, b):
            sp.dma_start(x_in[:, b, :], xs[bass.ds(j * P, P), :]).then_inc(x_loaded[b], 16)

        def store(j, b):
            sp.wait_ge(y_free, j + 2)
            sp.dma_start(ys[bass.ds(j * P, P), :], y_sb[:, b, :]).then_inc(y_stored[b], 16)

        sp.sem_inc(y_stored[0], 16)
        sp.sem_inc(y_stored[1], 16)
        load(0, 0)
        load(1, 1)
        with sp.Fori(0, n_loops - 1) as i:
            for b in range(2):
                j = 2 * i + b
                sp.wait_ge(xt_tp, j + 1)
                load(j + 2, b)
                store(j, b)
        sp.wait_ge(xt_tp, SLOT_TILES - 2)
        load(SLOT_TILES - 1, 0)
        for j in range(SLOT_TILES - 3, SLOT_TILES):
            store(j, j % 2)
        sp.wait_ge(y_stored[0], 16 + 16 * (n_loops + 1))
        sp.wait_ge(y_stored[1], 16 + 16 * n_loops)

    @block.scalar
    def _(act):
        def silu(j):
            act.wait_ge(g_ready, j + 1)
            for c in range(2):
                last = nc.scalar.activation(sg[:, c * FH:(c + 1) * FH], g_ps[c][:, 0:FH], ACT.Silu)
            last.then_inc(sg_ready, 1)

        def hidden_copy(j):
            act.wait_ge(ht_tp, j + 1)
            nc.scalar.activation(hT[:, 0:4, :].rearrange("p c t -> p (c t)"), ht_ps[0][:, :], ACT.Copy)
            nc.scalar.activation(hT[:, 4:FC, :].rearrange("p c t -> p (c t)"), ht_ps[1][:, 0:(FC - 4) * P],
                                 ACT.Copy).then_inc(ht_ready, 1)

        silu(0)
        with act.Fori(0, n_loops) as i:
            for b in range(2):
                j = 2 * i + 1 + b
                hidden_copy(j - 1)
                silu(j)
        hidden_copy(SLOT_TILES - 1)

    @block.vector
    def _(dve):
        def x_copy(j, b):
            dve.wait_ge(xt_tp, j + 1)
            nc.vector.tensor_copy(xT[:, b].rearrange("p k t -> p (k t)"), xt_ps[:, 0:KC * P]).then_inc(xt_ready, 1)

        def gated(j):
            dve.wait_ge(sg_ready, j + 1)
            dve.wait_ge(u_ready, j + 1)
            for c in range(2):
                last = nc.vector.tensor_tensor(hh[:, c * FH:(c + 1) * FH], u_ps[c][:, 0:FH],
                                               sg[:, c * FH:(c + 1) * FH], ALU.mult)
            last.then_inc(hh_ready, 1)

        def y_copy(j, b):
            dve.wait_ge(y_ready, j + 1)
            dve.wait_ge(y_stored[b], 16 * (j // 2 + 1) if isinstance(j, int) else 16 * y_index[0] + 16)
            nc.vector.tensor_copy(y_sb[:, b, :], y_ps[:, 0:DM]).then_inc(y_free, 1)

        y_index = [0]
        nc.vector.memset(hh[:, FF:FC * P], 0.0).then_inc(pad_zero, 1)
        dve.sem_inc(y_free, 1)
        x_copy(0, 0)
        gated(0)
        with dve.Fori(0, n_loops) as i:
            y_index[0] = i
            for b in range(2):
                j = 2 * i + 1 + b
                x_copy(j, 1 - b)
                gated(j)
                y_copy(j - 1, b)
        y_copy(SLOT_TILES - 1, 0)

    @block.tensor
    def _(pe):
        pe.wait_ge(weights_in, 16 * 4 * E)
        pe.wait_ge(tail_zero, 1)
        pe.wait_ge(pad_zero, 1)

        def x_transpose(j, b, i):
            pe.wait_ge(x_loaded[b], 16 * (i + 1))
            if not isinstance(j, int):
                pe.wait_ge(xt_ready, j)
            for kc in range(KC):
                mm = nc.tensor.transpose(xt_ps[:, kc * P:(kc + 1) * P], x_in[:, b, kc * P:(kc + 1) * P], ident[:])
            mm.then_inc(xt_tp, 1)

        def gate_up(j, b):
            e = nc.tensor.value_load(tile_expert[0:1, bass.ds(j, 1)], min_val=0, max_val=E - 1)
            pe.wait_ge(xt_ready, j + 1)
            for w, ps, ready in ((gate_sb, g_ps, g_ready), (up_sb, u_ps, u_ready)):
                for c in range(2):
                    for kc in range(KC):
                        mm = nc.tensor.matmul(ps[c][:, 0:FH], xT[:, b, kc, :],
                                              w[:, bass.ds(e, 1), kc, c * FH:(c + 1) * FH].rearrange("p o f -> p (o f)"),
                                              start=(kc == 0), stop=(kc == KC - 1))
                mm.then_inc(ready, 1)
            return e

        def hidden_transpose(j):
            pe.wait_ge(hh_ready, j + 1)
            for c in range(FC):
                mm = nc.tensor.transpose(ht_ps[c // 4][:, (c % 4) * P:(c % 4 + 1) * P], hh[:, c * P:(c + 1) * P], ident[:])
            mm.then_inc(ht_tp, 1)

        def down_proj(j):
            e = nc.tensor.value_load(tile_expert[0:1, bass.ds(j, 1)], min_val=0, max_val=E - 1)
            pe.wait_ge(ht_ready, j + 1)
            pe.wait_ge(y_free, j + 1)
            for c in range(FC):
                mm = nc.tensor.matmul(y_ps[:, 0:DM], hT[:, c, :],
                                      down_sb[:, bass.ds(e, 1), c, :].rearrange("p o d -> p (o d)"),
                                      start=(c == 0), stop=(c == FC - 1))
            mm.then_inc(y_ready, 1)

        x_transpose(0, 0, 0)
        gate_up(0, 0)
        with pe.Fori(0, n_loops) as i:
            for b in range(2):
                j = 2 * i + 1 + b
                x_transpose(j, 1 - b, i + b)
                hidden_transpose(j - 1)
                gate_up(j, 1 - b)
                down_proj(j - 1)
        hidden_transpose(SLOT_TILES - 1)
        down_proj(SLOT_TILES - 1)


def combine(nc, ctx, sbt, sem, h, ys, pos, gates, out):
    RING = 4
    y = sbt(ctx, "y_pair", [P, RING, TOPK, DM], F32)
    y_in = [sem(ctx, f"y_in{r}") for r in range(RING)]
    added, first, stored = sem(ctx, "added"), sem(ctx, "first"), sem(ctx, "stored")
    block = ctx.enter_context(nc.Block())

    @block.gpsimd
    def _(pool):
        for t in range(NT):
            if t >= RING:
                pool.wait_ge(added, t - RING + 1)
            for k in range(TOPK):
                nc.gpsimd.indirect_dma_start(
                    out=y[:, t % RING, k, :], out_offset=None, in_=ys,
                    in_offset=bass.IndirectOffsetOnAxis(ap=pos[:, k, t:t + 1], axis=0)).then_inc(y_in[t % RING], 16)

    @block.vector
    def _(dve):
        for t in range(NT):
            dve.wait_ge(y_in[t % RING], 32 * (t // RING + 1))
            nc.vector.scalar_tensor_tensor(h[:, t, :], y[:, t % RING, 0, :], gates[:, t, 0:1], h[:, t, :],
                                           ALU.mult, ALU.add).then_inc(first, 1)
            dve.wait_ge(first, t + 1)
            nc.vector.scalar_tensor_tensor(h[:, t, :], y[:, t % RING, 1, :], gates[:, t, 1:2], h[:, t, :],
                                           ALU.mult, ALU.add).then_inc(added, 1)

    @block.sync
    def _(sp):
        for t in range(NT):
            sp.wait_ge(added, t + 1)
            sp.dma_start(out[t * P:(t + 1) * P, :], h[:, t, :]).then_inc(stored, 16)
        sp.wait_ge(stored, 16 * NT)


def rope_tables():
    half = D // 2
    fraction = (np.float32(2.0) * np.arange(half, dtype=np.float32) / np.float32(D)).astype(np.float32)
    timescale = (np.float32(10000.0) ** fraction).astype(np.float32)
    angle = (np.arange(S, dtype=np.float32)[:, None] / timescale).astype(np.float32)
    sin, cos = np.sin(angle), np.cos(angle)
    scale = np.array([D ** -0.5, D ** -0.5, 1.0, 1.0], np.float32) / np.float32(W_SCALE)

    def lay(a):
        a = (a[:, None, :] * scale[None, :, None]).astype(np.float32)
        return np.ascontiguousarray(a.reshape(BT, P, 4, D).transpose(1, 0, 2, 3)).reshape(P, BT * 4 * D)

    return lay(np.concatenate([cos, cos], 1)), lay(np.concatenate([-sin, sin], 1))


def kernel(x, L0_tok_W, L0_attn_wqkv, L0_attn_wo, L0_ffn_router_w, L0_ffn_gate_w, L0_ffn_up_w, L0_ffn_down_w):
    import concourse.bacc as _bacc
    from concourse.bass_utils import run_bass_kernel_spmd as _run

    rope_c, rope_s = rope_tables()
    wqkv = np.asarray(L0_attn_wqkv).reshape(KC, P, 3, NP_, 128).transpose(1, 0, 3, 2, 4)

    def up_layout(w):
        return np.asarray(w).transpose(0, 2, 1).reshape(E, KC, P, FF).transpose(0, 2, 1, 3).reshape(E, P, KC * FF)

    arrays = {
        "ids": np.asarray(x).reshape(NT, P).T,
        "emb": np.asarray(L0_tok_W),
        "wqkv": wqkv.reshape(P, KC * NP_ * 384),
        "wo": np.asarray(L0_attn_wo).reshape(NP_, P, DM).transpose(1, 0, 2).reshape(P, NP_ * DM),
        "router": np.asarray(L0_ffn_router_w).T.reshape(KC, P, E).transpose(1, 0, 2).reshape(P, KC * E),
        "gate": up_layout(L0_ffn_gate_w),
        "up": up_layout(L0_ffn_up_w),
        "down": np.asarray(L0_ffn_down_w).transpose(0, 2, 1),
        "rope_c": rope_c,
        "rope_s": rope_s,
    }
    arrays = {name: np.ascontiguousarray(a) for name, a in arrays.items()}
    nc = _bacc.Bacc("TRN2", target_bir_lowering=False, num_devices=1)
    args = [nc.dram_tensor(name, a.shape, mybir.dt.from_np(a.dtype), kind="ExternalInput").ap()
            for name, a in arrays.items()]
    out = nc.dram_tensor("out", (T, DM), F32, kind="ExternalOutput").ap()
    program(nc, *args, out)
    r = _run(nc, [arrays], core_ids=[0])
    return r.results[0]["out"].reshape(B, S, DM)
```

```python
from contextlib import ExitStack

import numpy as np

import concourse.bass as bass
from concourse import mybir

ALU = mybir.AluOpType
ACT = mybir.ActivationFunctionType
AX = mybir.AxisListType
F32 = mybir.dt.float32
F16 = mybir.dt.float16
BF16 = mybir.dt.bfloat16
I32 = mybir.dt.int32
U32 = mybir.dt.uint32

P = 128
B, S, DM = 2, 1024, 256
H, D = 16, 64
E, FF, TOPK = 8, 704, 2
T = B * S
NT = T // P
BT = S // P
GT = 4
NG = NT // GT
KC = DM // P
NP_ = H // 2
NU = B * NP_
FC = -(-FF // P)
FH = FF // 2
SLOT_TILES = TOPK * T // P + E - 1
ROW = DM + 1
EPS = 1e-5
STAGES = 4
XB = 2
POOL_MATRICES = tuple(range(9))
DVE_EARLY = 0
HIGHS_UNTIL = (1, 2, 3, 4, 5)
MATRICES = 3 * E
DVE_MATRICES = tuple(m for m in range(MATRICES) if m not in POOL_MATRICES)
W_SCALE = 64.0
M_SCALE = 64.0
NEG = -1.0e10

PIECES = []
_col = 0
for _half in range(2):
    for _kt in range(4 * (_half + 1)):
        _q = max(_kt * P, 512 * _half)
        PIECES.append((_kt, _q, 512 * (_half + 1) - _q, _col))
        _col += 512 * (_half + 1) - _q
PCOLS = _col
NPC = len(PIECES)
SLOTS = 2 * NPC
RING = 4
MPIECES = [(qt, hh, hf, min(512, (qt + 1) * P - 512 * hf))
           for qt in range(BT) for hh in range(2) for hf in range(1 if qt < 4 else 2)]
NMP = len(MPIECES)
MAX_AT = {5: (0, 1), 7: (2, 3), 9: (4, 5), 11: (6, 7), 13: (8, 9), 14: (10, 11), 15: (12, 13), 16: (14, 15),
          17: (16, 17), 18: (18, 19), 19: (20, 21), 20: (22, 23)}
MAX_ROWS_AT = 21
VALUES_AT = {6: (0, (0, 1, 2, 3)), 12: (0, (4,)), 13: (0, (5,)), 15: (0, (6,)), 16: (0, (7,)),
             21: (1, (0, 1, 2, 3)), 23: (1, (4,))}
CONTEXT_AT = {0: 0, 2: 1}
OUTPUT_AT = {2: 0, 3: 1, 5: 2, 6: 3}
PROJECT_AT = {0: 0, 2: 1, 4: 2, 6: 3, 8: 4, 10: 5, 12: 6, 14: 7}
PACK_AT = {3: 0, 5: 1, 6: 2, 9: 3, 11: 4, 13: 5, 15: 6, 17: 7}
SIDE = []
for _s in range(SLOTS):
    SIDE += [("max", i) for i in MAX_AT.get(_s, ())[:1]] + [("output", j) for at, j in OUTPUT_AT.items() if at == _s]
    SIDE += [("max", i) for i in MAX_AT.get(_s, ())[1:]]
Q_AT = [0, 5 * D]
K_AT = [2 * D, 7 * D]
HALVES = 10 * D
TP_USES = BT + 1 + 2


def first(n):
    return isinstance(n, int) and n == 0


def before_pack(n, t):
    return t if first(n) else TP_USES * n - 2 + t


def before_maxima(n):
    return before_pack(n, BT)


def before_context(n, g):
    return (TP_USES * n + 2 * (BT + 1) if not (isinstance(n, int) and n == NU - 1) else TP_USES * n + BT + 1) + g


def side_use(n, kind, i):
    order, base = SIDE, len(SIDE) * (n - 1) + 2 * NMP
    if isinstance(n, int) and n <= 0:
        order, base = [u for u in SIDE if u[0] == "max"], NMP * (n + 1)
    if isinstance(n, int) and n >= NU - 1:
        order = [u for u in SIDE if u[0] == "output"]
        base = len(SIDE) * (NU - 2) + 2 * NMP + len(order) * (n - NU + 1)
    return base + order.index((kind, i)), order.index((kind, i)) % 2


def program(nc, ids, emb, wqkv, wo, router, gate, up, down, rope_c, rope_s, out):
    xs = nc.dram_tensor("slot_x", (SLOT_TILES * P, ROW), F32).ap()
    ys = nc.dram_tensor("choice_y", (TOPK * T + P, DM), F32).ap()
    top = ExitStack()
    with top:
        def sbt(ctx, name, shape, dt):
            return ctx.enter_context(nc.sbuf_tensor(name, shape, dt))

        def sem(ctx, name):
            return ctx.enter_context(nc.semaphore(name))

        h = sbt(top, "h", [P, NT, DM], F32)
        ident = sbt(top, "ident", [P, P], F32)
        stats = sbt(top, "stats", [P, GT, 6], F32)
        mv = sbt(top, "mv", [P, NT, 2], F32)
        veps = sbt(top, "veps", [P, NT], F32)
        std = sbt(top, "std", [P, NT], F32)
        rstd = sbt(top, "rstd", [P, NT], F32)
        w_in = sbt(top, "w_in", [P, STAGES, FC * DM], F32)
        w_loaded = [sem(top, f"w_loaded{r}") for r in range(STAGES)]
        banks = [top.enter_context(nc.psum_tensor(f"bank{i}", [P, 512], F32)) for i in range(8)]

        attention(nc, sbt, sem, h, ident, (stats, mv, veps, std, rstd), banks,
                  ids, emb, wqkv, wo, rope_c, rope_s, xs, w_in, w_loaded, (gate, up, down))
        experts(nc, sbt, sem, h, ident, (stats, mv, veps, std, rstd), banks,
                router, (gate, up, down), xs, ys, out, w_in, w_loaded)


def row_stats(nc, dve, g, stat_done, var_ready, h, norm, before=0):
    stats, mv, veps, std, rstd = norm
    for i in range(GT):
        nc.vector.bn_stats(stats[:, i, :], h[:, GT * g + i, :]).then_inc(stat_done, 1)
    dve.wait_ge(stat_done, 2 * GT * (before + g) + GT)
    for i in range(GT):
        nc.vector.bn_aggr(mv[:, GT * g + i, :], stats[:, i, :]).then_inc(stat_done, 1)
    dve.wait_ge(stat_done, 2 * GT * (before + g + 1))
    nc.vector.tensor_scalar(veps[:, GT * g:GT * (g + 1)], mv[:, GT * g:GT * (g + 1), 1], EPS, None,
                            ALU.add).then_inc(var_ready, 1)


def row_roots(nc, act, g, var_ready, std_ready, norm, before=0):
    stats, mv, veps, std, rstd = norm
    if var_ready is not None:
        act.wait_ge(var_ready, before + g + 1)
    nc.scalar.activation(std[:, GT * g:GT * (g + 1)], veps[:, GT * g:GT * (g + 1)], ACT.Sqrt).then_inc(std_ready, 1)


def normal_rows(nc, dve, g, std_ready, rstd_ready, xn_ready, rows, h, norm):
    stats, mv, veps, std, rstd = norm
    dve.wait_ge(std_ready, g + 1)
    nc.vector.reciprocal(rstd[:, GT * g:GT * (g + 1)], std[:, GT * g:GT * (g + 1)]).then_inc(rstd_ready, 1)
    dve.wait_ge(rstd_ready, g + 1)
    for t in range(GT * g, GT * (g + 1)):
        nc.vector.tensor_scalar(rows(t), h[:, t, :], mv[:, t, 0:1], rstd[:, t:t + 1],
                                ALU.subtract, ALU.mult).then_inc(xn_ready, 1)


def load_matrix(sp, m, w_in, w_loaded, weights):
    gate, up, down = weights
    e, r = m // 3, m % STAGES
    if m % 3 < 2:
        sp.dma_start(w_in[:, r, 0:KC * FF], (gate, up)[m % 3][e]).then_inc(w_loaded[r], 16)
    else:
        full = FF // P
        sp.dma_start(w_in[:, r, 0:full * DM].rearrange("p (c d) -> p c d", c=full),
                     down[e, 0:full * P, :].rearrange("(c p) d -> p c d", p=P)).then_inc(w_loaded[r], 16)
        sp.dma_start(w_in[0:FF % P, r, full * DM:], down[e, full * P:FF, :]).then_inc(w_loaded[r], 16)


def attention(nc, sbt, sem, h, ident, norm, banks, ids, emb, wqkv, wo, rope_c, rope_s, xs,
              w_in, w_loaded, weights):
    stats, mv, veps, std, rstd = norm
    ctx = ExitStack()
    with ctx:
        def sb(name, shape, dt):
            return sbt(ctx, name, shape, dt)

        def sm(name):
            return sem(ctx, name)

        ids_sb = sb("ids_sb", [P, NT], I32)
        ident16 = sb("ident16", [P, P], F16)
        identb = sb("identb", [P, P], BF16)
        mask_q = sb("mask_q", [P, P], BF16)
        mask_k = sb("mask_k", [P, P], BF16)
        zeros = sb("zeros", [P, ROW], F32)
        xn = sb("xn", [P, 4, DM], F32)
        x16 = sb("x16", [P, 4, 2, DM], F16)
        xT = sb("xT", [P, 2, KC, T], F16)
        w16 = w_in[:, :, :].rearrange("p r c -> p (r c)").bitcast(F16)[:, 0:2 * KC * NP_ * 384].rearrange(
            "p (a k u c) -> p a k u c", a=2, k=KC, u=NP_)
        wo_sb = sb("wo_sb", [P, NP_, DM], F32)
        wo16 = sb("wo16", [P, 2, NP_, DM], F16)
        rc = sb("rc", [P, BT, 4, D], F32)
        rs = sb("rs", [P, BT, 4, D], F32)
        rope_a = sb("rope_a", [P, 2, 4, D], F32)
        rope_b = sb("rope_b", [P, 2, 4, D], F32)
        roped = sb("roped", [P, 2, 4, D], F32)
        maskf = rope_a[:, 0].rearrange("p (m a) d -> p m (a d)", m=2)
        halves = sb("halves", [P, 2, HALVES], F16)
        stack = sb("stack", [P, B, 4, S], F16)
        aug = sb("aug", [65, B, 4, S], F16)
        v = sb("v", [P, 2, B, BT, 2, D + 1], F16)
        probs = sb("probs", [P, 2, PCOLS], F32)
        p32 = sb("p32", [P, RING, 512], F32)
        mx = sb("mx", [P, 2, 16], F32)
        mneg = sb("mneg", [P, 2, 16], F32)
        m16 = sb("m16", [P, 16], F16)
        mT = sb("mT", [16, P], F16)
        rsum = sb("rsum", [P, 4], F32)
        cx = sb("cx", [P, BT, 2, D], F32)
        cT = sb("cT", [P, 2, 2, 512], F16)

        p16 = [probs[:, a, :].bitcast(F16).rearrange("p (h c) -> p h c", h=2) for a in range(2)]
        w32 = probs[:, :, :].rearrange("p a c -> p (a c)")[:, 0:KC * NP_ * 384].rearrange("p (k u c) -> p k u c", k=KC, u=NP_)
        xT_all = xT[:, :, :, :].rearrange("p a k t -> p (a k) t")

        qkv_ps = [banks[0], banks[7]]
        tp_ps = banks[1]
        tp16 = tp_ps[:, :].bitcast(F16)
        side_ps = banks[2:4]
        st_ps = banks[4:6]
        ctx_ps = banks[6]

        s_ids, s_zero, s_fill = sm("s_ids"), sm("s_zero"), sm("s_fill")
        s_emb = [sm(f"s_emb{g}") for g in range(NG)]
        s_rope_tab, s_wqkv, s_wo = sm("s_rope_tab"), sm("s_wqkv"), sm("s_wo")
        s_c, s_const = sm("s_c"), sm("s_const")
        s_whi, s_wlo = sm("s_whi"), sm("s_wlo")
        s_stat, s_var, s_std, s_rstd = sm("s_stat"), sm("s_var"), sm("s_std"), sm("s_rstd")
        s_xn, s_xhi, s_xlo = sm("s_xn"), sm("s_xhi"), sm("s_xlo")
        s_xtp, s_xT = sm("s_xtp"), sm("s_xT")
        s_setup, wo_high_ready, wo_low_ready, cx_high_ready = (
            sm("s_setup"), sm("wo_high_ready"), sm("wo_low_ready"), sm("cx_high_ready"))
        qkv_ready, rope_terms, roped_ready = sm("qkv_ready"), sm("rope_terms"), sm("roped_ready")
        hi_ready, lo_ready, twice_ready = sm("hi_ready"), sm("lo_ready"), sm("twice_ready")
        vhi_ready, qkv_free = sm("vhi_ready"), sm("qkv_free")
        pack_tp, max_tp, ctx_tp, tp_free = sm("pack_tp"), sm("max_tp"), sm("ctx_tp"), sm("tp_free")
        max_ready, y_ready, side_free = sm("max_ready"), sm("y_ready"), sm("side_free")
        mneg_ready, m16_ready, mrow_ready = sm("mneg_ready"), sm("m16_ready"), sm("mrow_ready")
        st_ready, st_free, plo_done = sm("st_ready"), sm("st_free"), sm("plo_done")
        pv_ready, rsum_ready, ctx_free = sm("pv_ready"), sm("rsum_ready"), sm("ctx_free")

        block = ctx.enter_context(nc.Block())

        @block.sync
        def _(sp):
            sp.dma_start(ids_sb[:], ids).then_inc(s_ids, 16)
            sp.dma_start(w32.rearrange("p k u c -> p (k u c)"), wqkv).then_inc(s_wqkv, 16)
            for g in range(NG):
                sp.wait_ge(s_emb[g], 16 * GT)
            sp.dma_start(rc[:, :, :, :].rearrange("p t a d -> p (t a d)"), rope_c).then_inc(s_rope_tab, 16)
            sp.dma_start(rs[:, :, :, :].rearrange("p t a d -> p (t a d)"), rope_s).then_inc(s_rope_tab, 16)
            sp.dma_start(wo_sb[:, :, :].rearrange("p u n -> p (u n)"), wo).then_inc(s_wo, 16)

            def max_row(n, b):
                sp.wait_ge(tp_free, before_maxima(n) + 1)
                for hh in range(2):
                    sp.dma_start(aug[64:65, b, hh, :],
                                 mT[8 * hh:8 * hh + 8, :]).then_inc(mrow_ready, 16)

            max_row(0, 0)
            sp.wait_ge(s_zero, 2)
            sp.dma_start(xs.rearrange("(r p) d -> p r d", p=P),
                         zeros[:, :].unsqueeze(1).to_broadcast([P, SLOT_TILES, ROW])).then_inc(s_fill, 16)
            with sp.Fori(0, NP_ - 1) as p:
                max_row(2 * p + 1, 1)
                max_row(2 * p + 2, 0)
            max_row(NU - 1, 1)
            sp.wait_ge(qkv_ready, BT * NU)
            for m in range(STAGES):
                load_matrix(sp, m, w_in, w_loaded, weights)
            sp.wait_ge(s_fill, 16)

        @block.gpsimd
        def _(pool):
            nc.gpsimd.memset(zeros[:, 0:DM], 0.0).then_inc(s_zero, 1)
            nc.gpsimd.iota(zeros[:, DM:ROW].bitcast(I32), pattern=[[1, 1]], base=TOPK * T,
                           channel_multiplier=1).then_inc(s_zero, 1)
            nc.gpsimd.memset(ident[:], 0.0).then_inc(s_c, 1)
            nc.gpsimd.memset(maskf, 0.0).then_inc(s_c, 1)

            def gather(t):
                nc.gpsimd.indirect_dma_start(
                    out=h[:, t, :], out_offset=None, in_=emb,
                    in_offset=bass.IndirectOffsetOnAxis(ap=ids_sb[:, t:t + 1], axis=0)).then_inc(s_emb[t // GT], 16)

            pool.wait_ge(s_ids, 16)
            for t in range(2 * GT):
                gather(t)
            pool.wait_ge(s_c, 2)
            nc.gpsimd.affine_select(out=ident[:], in_=ident[:], compare_op=ALU.not_equal, fill=1.0, base=0,
                                    pattern=[[-1, P]], channel_multiplier=1).then_inc(s_c, 1)
            nc.gpsimd.affine_select(out=maskf[:, 0, :], in_=maskf[:, 0, :], compare_op=ALU.is_ge, fill=NEG, base=0,
                                    pattern=[[-1, P]], channel_multiplier=1).then_inc(s_c, 1)
            nc.gpsimd.affine_select(out=maskf[:, 1, :], in_=maskf[:, 1, :], compare_op=ALU.is_ge, fill=NEG, base=0,
                                    pattern=[[1, P]], channel_multiplier=-1).then_inc(s_c, 1)
            pool.wait_ge(s_c, 5)
            nc.gpsimd.tensor_copy(ident16[:], ident[:]).then_inc(s_const, 1)
            nc.gpsimd.tensor_copy(identb[:], ident[:]).then_inc(s_const, 1)
            nc.gpsimd.tensor_copy(mask_q[:], maskf[:, 0, :]).then_inc(s_const, 1)
            nc.gpsimd.tensor_copy(mask_k[:], maskf[:, 1, :]).then_inc(s_const, 1)
            for t in range(2 * GT, NT):
                gather(t)
            def low_halves(n, s):
                kt, q, w, c = PIECES[s % NPC]
                pool.wait_ge(st_free, 2 + SLOTS * n + s + 1)
                nc.gpsimd.tensor_tensor(p16[1][:, s // NPC, c:c + w], p32[:, s % RING, 0:w],
                                        p16[0][:, s // NPC, c:c + w], ALU.subtract).then_inc(plo_done, 1)

            def rope_sum(n, t):
                g = BT * n + t
                pool.wait_ge(rope_terms, 2 * g + 2)
                if not (isinstance(g, int) and g < 2):
                    pool.wait_ge(lo_ready, g - 1)
                nc.gpsimd.tensor_tensor(roped[:, t % 2], rope_a[:, t % 2], rope_b[:, t % 2],
                                        ALU.add).then_inc(roped_ready, 1)

            def weights_low(u):
                pool.wait_ge(s_whi, u + 1)
                nc.gpsimd.tensor_tensor(w16[:, 1, :, u], w32[:, :, u], w16[:, 0, :, u], ALU.subtract).then_inc(s_wlo, 1)

            weights_low(0)
            pool.sem_inc(plo_done, RING)
            for t in range(BT):
                rope_sum(0, t)
                if t > 0:
                    weights_low(t)
            with pool.Fori(0, NU - 1) as n:
                for s in range(SLOTS):
                    if s in PROJECT_AT:
                        rope_sum(n + 1, PROJECT_AT[s])
                    low_halves(n, s)
            for s in range(SLOTS):
                low_halves(NU - 1, s)

        @block.scalar
        def _(act):
            act.sem_inc(s_xT, 2)
            def weights_high(u):
                nc.scalar.activation(w16[:, 0, :, u], w32[:, :, u], ACT.Copy, scale=W_SCALE)
                nc.scalar.activation(w32[:, :, u], w32[:, :, u], ACT.Copy, scale=W_SCALE).then_inc(s_whi, 1)

            row_roots(nc, act, 0, s_var, s_std, norm)
            for g in range(NG):
                for i in range(GT):
                    act.wait_ge(s_xn, GT * g + i + 1)
                    if g > 0:
                        act.wait_ge(s_xtp, GT * (g - 1) + i + 1)
                    nc.scalar.activation(x16[:, i, 0, :], xn[:, i, :], ACT.Copy).then_inc(s_xhi, 1)
                if g + 1 < NG:
                    row_roots(nc, act, g + 1, s_var, s_std, norm)
                if g == NG - 2:
                    act.wait_ge(s_wqkv, 16)
                    weights_high(0)
                for i in range(GT):
                    t = GT * g + i
                    act.wait_ge(s_xtp, t + 1)
                    nc.scalar.activation(xT_all[:, :, P * t:P * (t + 1)],
                                         banks[i % 2][:, :].bitcast(F16)[:, 0:512].rearrange("p (a t) -> p a t", a=4),
                                         ACT.Copy).then_inc(s_xT, 1)


            def value_high(n, b, t):
                act.wait_ge(rope_terms, 2 * (BT * n + t) + 2)
                nc.scalar.activation(v[:, 0, b, t, :, 0:D],
                                     qkv_ps[t % 2][:, 256:384].rearrange("p (h d) -> p h d", h=2),
                                     ACT.Copy).then_inc(vhi_ready, 1)

            def keys_twice(n, t):
                act.wait_ge(hi_ready, BT * n + t + 1)
                k = halves[:, t % 2].rearrange("p (a c) -> p a c", a=2)
                nc.scalar.activation(k[:, :, K_AT[0] + D:K_AT[0] + 2 * D], k[:, :, K_AT[0]:K_AT[0] + D],
                                     ACT.Copy).then_inc(twice_ready, 1)

            def stacks(n, b, t):
                act.wait_ge(pack_tp, BT * n + t + 1)
                nc.scalar.activation(stack[:, b, :, t * P:(t + 1) * P],
                                     tp16[:, 0:512].rearrange("p (a t) -> p a t", a=4), ACT.Copy)
                nc.scalar.activation(aug[0:64, b, :, t * P:(t + 1) * P],
                                     tp16[0:64, 256:768].rearrange("p (a t) -> p a t", a=4),
                                     ACT.Copy).then_inc(tp_free, 1)

            def exps(n, s):
                kt, q, w, c = PIECES[s % NPC]
                act.wait_ge(st_ready, SLOTS * n + s + 1)
                act.wait_ge(plo_done, SLOTS * n + s + 1)
                nc.scalar.activation(p32[:, s % RING, 0:w], st_ps[s % 2][:, 0:w], ACT.Exp)
                nc.scalar.activation(p16[0][:, s // NPC, c:c + w], st_ps[s % 2][:, 0:w],
                                     ACT.Exp).then_inc(st_free, 1)

            def maxima(n):
                act.wait_ge(max_tp, n + 1)
                nc.scalar.activation(mT[:], tp16[0:16, 0:P], ACT.Copy).then_inc(tp_free, 1)

            def context(n, g):
                act.wait_ge(ctx_tp, 2 * n + g + 1)
                nc.scalar.activation(cT[:, 0, g, :], tp_ps[:, :], ACT.Copy).then_inc(cx_high_ready, 1)

            def unit(n, b, prev, nxt):
                for s in range(SLOTS):
                    exps(n, s)
                    if prev and s in CONTEXT_AT:
                        context(n - 1, CONTEXT_AT[s])
                    if nxt:
                        if s - 1 in PROJECT_AT:
                            value_high(n + 1, 1 - b, PROJECT_AT[s - 1])
                        if s in PACK_AT:
                            stacks(n + 1, 1 - b, PACK_AT[s])
                        if s - 1 in PROJECT_AT:
                            keys_twice(n + 1, PROJECT_AT[s - 1])
                        if s == MAX_ROWS_AT:
                            maxima(n + 1)

            act.sem_inc(st_free, 2)
            for t in range(BT + 2):
                if t < BT:
                    value_high(0, 0, t)
                if 1 <= t <= BT:
                    keys_twice(0, t - 1)
                if t < NP_ - 1:
                    weights_high(t + 1)
                if t >= 2:
                    stacks(0, 0, t - 2)
            act.wait_ge(s_wo, 16)
            nc.scalar.activation(wo16[:, 0], wo_sb[:], ACT.Copy, scale=W_SCALE).then_inc(wo_high_ready, 1)
            maxima(0)
            unit(0, 0, False, True)
            with act.Fori(0, NP_ - 1) as p:
                unit(2 * p + 1, 1, True, True)
                unit(2 * p + 2, 0, True, True)
            unit(NU - 1, 1, True, False)
            for g in range(2):
                context(NU - 1, g)

        @block.tensor
        def _(pe):
            pe.wait_ge(s_const, 4)
            for t in range(NT):
                i = t % GT
                pe.wait_ge(s_xlo, t + 1)
                pe.wait_ge(s_xT, t + 1)
                for a in range(4):
                    mm = nc.tensor.transpose(banks[t % 2][:, :].bitcast(F16)[:, a * P:(a + 1) * P],
                                             x16[:, i, a // 2, (a % 2) * P:(a % 2 + 1) * P], ident16[:])
                mm.then_inc(s_xtp, 1)
            pe.wait_ge(s_xT, NT + 2)
            pe.wait_ge(s_wlo, 1)

            def project(n, p, b, t):
                i = BT * n + t
                if not (isinstance(i, int) and i < 2):
                    pe.wait_ge(qkv_free, i - 1)
                tok = S * b + P * t
                for kc in range(KC):
                    for a, c in ((0, 0), (0, 1), (1, 0)):
                        mm = nc.tensor.matmul(qkv_ps[t % 2][:, 0:384], xT[:, a, kc, tok:tok + P],
                                              w16[:, c, kc, bass.ds(p, 1), :].rearrange("p o c -> p (o c)"),
                                              start=(kc == 0 and a == 0 and c == 0), stop=(kc == KC - 1 and a == 1))
                mm.then_inc(qkv_ready, 1)

            def pack(n, t):
                i = t % 2
                pe.wait_ge(lo_ready, BT * n + t + 1)
                pe.wait_ge(twice_ready, BT * n + t + 1)
                w = before_pack(n, t)
                if not (isinstance(w, int) and w == 0):
                    pe.wait_ge(tp_free, w)
                for hh in range(2):
                    k, q = K_AT[hh], Q_AT[hh]
                    nc.tensor.transpose(tp16[:, hh * P:(hh + 1) * P], halves[:, i, k:k + 2 * D], ident16[:])
                    nc.tensor.transpose(tp16[:, (2 + hh) * P:(3 + hh) * P], halves[:, i, q:q + 2 * D], ident16[:])
                    mm = nc.tensor.transpose(tp16[0:D, (4 + hh) * P:(5 + hh) * P],
                                             halves[:, i, k + 2 * D:k + 3 * D], ident16[:])
                mm.then_inc(pack_tp, 1)

            def max_piece(n, b, i):
                qt, hh, hf, w = MPIECES[i]
                u, bank = side_use(n - 1, "max", i)
                if not (isinstance(u, int) and u < 2):
                    pe.wait_ge(side_free, u - 1)
                pe.wait_ge(tp_free, before_pack(n, qt) + 1)
                diag = qt // 4 == hf
                ps = side_ps[bank]
                mm = nc.tensor.matmul(ps[:, 0:w], stack[:, b, 2 + hh, qt * P:(qt + 1) * P],
                                      stack[:, b, hh, 512 * hf:512 * hf + w], start=True, stop=not diag)
                if diag:
                    mm = nc.tensor.matmul(ps[:, w - P:w], identb[:], mask_q[:], start=False, stop=True)
                mm.then_inc(max_ready, 1)

            def max_rows(n):
                pe.wait_ge(m16_ready, n + 1)
                pe.wait_ge(tp_free, before_maxima(n))
                nc.tensor.transpose(tp16[0:16, 0:P], m16[:], ident16[:]).then_inc(max_tp, 1)

            def scores(n, b, s):
                kt, q, w, c = PIECES[s % NPC]
                hh = s // NPC
                pe.wait_ge(st_free, SLOTS * n + s + 1)
                ps = st_ps[s % 2]
                nc.tensor.matmul(ps[:, 0:w], stack[:, b, hh, kt * P:(kt + 1) * P], stack[:, b, 2 + hh, q:q + w],
                                 start=True, stop=False)
                mm = nc.tensor.matmul(ps[:, 0:w], aug[0:65, b, 2 + hh, kt * P:(kt + 1) * P],
                                      aug[0:65, b, hh, q:q + w], start=False, stop=(q != kt * P))
                if q == kt * P:
                    mm = nc.tensor.matmul(ps[:, 0:P], identb[:], mask_k[:], start=False, stop=True)
                mm.then_inc(st_ready, 1)

            def values(n, b, hh, tiles):
                half = tiles[0] // 4
                if tiles[0] % 4 == 0:
                    pe.wait_ge(qkv_free, BT * (n + 1))
                    pe.wait_ge(ctx_free, 4 * n + 2 * hh + half + 1)
                for qt in tiles:
                    last = NPC * hh + 4 * half + qt
                    pe.wait_ge(plo_done, RING + SLOTS * n + last + 1)
                    acc = ctx_ps[:, (qt % 4) * 65:(qt % 4) * 65 + 65]
                    for kt in range(qt + 1):
                        c = [c + P * qt - q for k, q, w, c in PIECES if k == kt and q <= P * qt < q + w][0]
                        for a, d in ((0, 0), (0, 1), (1, 0)):
                            mm = nc.tensor.matmul(acc, p16[a][:, hh, c:c + P], v[:, d, b, kt, hh, :],
                                                  start=(kt == 0 and a == 0 and d == 0), stop=(kt == qt and a == 1))
                if tiles[-1] % 4 == 3:
                    mm.then_inc(pv_ready, 1)

            def context(n, g):
                pe.wait_ge(ctx_free, 1 + 4 * n + 3 + g)
                pe.wait_ge(tp_free, before_context(n, g))
                for i in range(4):
                    mm = nc.tensor.transpose(tp_ps[:, i * P:(i + 1) * P],
                                             cx[:, 4 * g + i].rearrange("p h d -> p (h d)"), ident[:])
                mm.then_inc(ctx_tp, 1)

            def output(n, p, j):
                if j % 2 == 0:
                    pe.wait_ge(tp_free, before_context(n, j // 2) + 1)
                u, bank = side_use(n + 1, "output", j)
                pe.wait_ge(side_free, u - 1)
                for i in range(2):
                    t = 2 * j + i
                    for a, d in ((0, 0), (0, 1), (1, 0)):
                        mm = nc.tensor.matmul(side_ps[bank][:, i * DM:(i + 1) * DM],
                                              cT[:, a, t // 4, (t % 4) * P:(t % 4 + 1) * P],
                                              wo16[:, d, bass.ds(p, 1), :].rearrange("p o c -> p (o c)"),
                                              start=(a == 0 and d == 0), stop=(a == 1))
                mm.then_inc(y_ready, 1)

            def unit(n, p, b, prev, nxt):
                pe.wait_ge(mrow_ready, 32 * (n + 1))
                for s in range(SLOTS):
                    scores(n, b, s)
                    if nxt:
                        for i in MAX_AT.get(s, ())[:1]:
                            max_piece(n + 1, 1 - b, i)
                    if nxt and s in PROJECT_AT:
                        project(n + 1, p + b, 1 - b, PROJECT_AT[s])
                    if prev and s in CONTEXT_AT:
                        context(n - 1, CONTEXT_AT[s])
                    if prev and s in OUTPUT_AT:
                        output(n - 1, p + b - 1, OUTPUT_AT[s])
                    if nxt and s in PACK_AT:
                        pack(n + 1, PACK_AT[s])
                    if s in VALUES_AT:
                        values(n, b, *VALUES_AT[s])
                    if nxt:
                        for i in MAX_AT.get(s, ())[1:]:
                            max_piece(n + 1, 1 - b, i)
                        if s == MAX_ROWS_AT:
                            max_rows(n + 1)
                values(n, b, 1, (5, 6, 7))

            for t in range(BT + 3):
                if t < BT:
                    project(0, 0, 0, t)
                if 2 <= t <= BT + 1:
                    pack(0, t - 2)
                for i in range(NMP):
                    if MPIECES[i][0] == t - 3:
                        max_piece(0, 0, i)
            max_rows(0)
            pe.wait_ge(s_setup, 4)
            pe.wait_ge(s_wlo, NP_)
            unit(0, 0, 0, False, True)
            pe.wait_ge(wo_low_ready, 1)
            with pe.Fori(0, NP_ - 1) as p:
                unit(2 * p + 1, p, 1, True, True)
                unit(2 * p + 2, p + 1, 0, True, True)
            unit(NU - 1, NP_ - 1, 1, True, False)
            for g in range(2):
                context(NU - 1, g)
                output(NU - 1, NP_ - 1, 2 * g)
                output(NU - 1, NP_ - 1, 2 * g + 1)

        @block.vector
        def _(dve):
            nc.vector.memset(aug[64:65, :, 2:4, :], M_SCALE).then_inc(s_setup, 1)
            nc.vector.memset(v[:, 0, :, :, :, D:D + 1], 1.0).then_inc(s_setup, 1)
            nc.vector.memset(v[:, 1, :, :, :, D:D + 1], 0.0).then_inc(s_setup, 1)
            nc.vector.memset(mx[:, 1, :], -3.0e38).then_inc(s_setup, 1)
            dve.wait_ge(s_setup, 4)

            def start_stats(g):
                dve.wait_ge(s_emb[g], 16 * GT)
                row_stats(nc, dve, g, s_stat, s_var, h, norm)

            start_stats(0)
            for g in range(NG):
                normal_rows(nc, dve, g, s_std, s_rstd, s_xn, lambda t: xn[:, t % GT, :], h, norm)
                if g + 1 < NG:
                    start_stats(g + 1)
                for t in range(GT * g, GT * (g + 1)):
                    dve.wait_ge(s_xhi, t + 1)
                    nc.vector.tensor_tensor(x16[:, t % GT, 1, :], xn[:, t % GT, :], x16[:, t % GT, 0, :],
                                            ALU.subtract).then_inc(s_xlo, 1)

            dve.wait_ge(s_rope_tab, 32)

            def rope_products(n, t):
                i = t % 2
                ps = qkv_ps[i]
                dve.wait_ge(qkv_ready, BT * n + t + 1)
                if not (isinstance(n, int) and n == 0 and t < 2):
                    dve.wait_ge(roped_ready, BT * n + t - 1)
                qk = ps[:, 0:256].rearrange("p (a d) -> p a d", a=4)
                nc.vector.tensor_tensor(rope_a[:, i], qk, rc[:, t], ALU.mult).then_inc(rope_terms, 1)
                swapped = bass.AP(ps, D // 2, [[512, P], [D, 4], [-(D // 2), 2], [1, D // 2]])
                nc.vector.tensor_tensor(rope_b[:, i].rearrange("p a (s d) -> p a s d", s=2), swapped,
                                        rs[:, t].rearrange("p a (s d) -> p a s d", s=2),
                                        ALU.mult).then_inc(rope_terms, 1)

            def places(t, low):
                return bass.AP(halves, HALVES * (t % 2) + D * low,
                               [[2 * HALVES, P], [K_AT[0] + D * low, 2], [5 * D, 2], [1, D]])

            def rotated(t):
                return roped[:, t % 2].rearrange("p (a h) d -> p a h d", a=2)

            def high(n, t):
                g = BT * n + t
                dve.wait_ge(roped_ready, g + 1)
                if not (isinstance(g, int) and g < 2):
                    dve.wait_ge(pack_tp, g - 1)
                nc.vector.tensor_copy(places(t, 0), rotated(t)).then_inc(hi_ready, 1)

            def low(n, t):
                dve.wait_ge(hi_ready, BT * n + t + 1)
                nc.vector.tensor_tensor(places(t, 1), rotated(t), places(t, 0), ALU.subtract).then_inc(lo_ready, 1)

            def value_low(n, b, t):
                dve.wait_ge(vhi_ready, BT * n + t + 1)
                nc.vector.tensor_tensor(v[:, 1, b, t, :, 0:D],
                                        qkv_ps[t % 2][:, 256:384].rearrange("p (h d) -> p h d", h=2),
                                        v[:, 0, b, t, :, 0:D], ALU.subtract).then_inc(qkv_free, 1)

            def maximum(n, i):
                qt, hh, hf, w = MPIECES[i]
                dve.wait_ge(max_ready, NMP * n + i + 1)
                bank = side_use(n - 1, "max", i)[1]
                nc.vector.reduce_max(mx[:, hf, 8 * hh + qt:8 * hh + qt + 1], side_ps[bank][:, 0:w],
                                     AX.X).then_inc(side_free, 1)

            def negate(n):
                dve.wait_ge(side_free, side_use(n - 1, "max", NMP - 1)[0] + 1)
                nc.vector.tensor_scalar(mneg[:], mx[:], -1.0 / M_SCALE, None, ALU.mult).then_inc(mneg_ready, 1)
                dve.wait_ge(mneg_ready, n + 1)
                nc.vector.tensor_tensor(m16[:], mneg[:, 0, :], mneg[:, 1, :], ALU.min).then_inc(m16_ready, 1)

            def normalize(n, hh, g):
                i = 4 * n + 2 * hh + g
                acc = ctx_ps[:, 0:260].rearrange("p (q d) -> p q d", q=4)
                dve.wait_ge(pv_ready, i + 1)
                nc.vector.reciprocal(rsum[:], acc[:, :, D]).then_inc(rsum_ready, 1)
                dve.wait_ge(rsum_ready, i + 1)
                nc.vector.tensor_tensor(cx[:, 4 * g:4 * g + 4, hh, :], acc[:, :, 0:D],
                                        rsum[:, :].unsqueeze(2).to_broadcast([P, 4, D]),
                                        ALU.mult).then_inc(ctx_free, 1)

            def residual(n, b, j):
                dve.wait_ge(y_ready, 4 * n + j + 1)
                rows = h[:, BT * b + 2 * j:BT * b + 2 * j + 2, :]
                bank = side_use(n + 1, "output", j)[1]
                nc.vector.scalar_tensor_tensor(rows, side_ps[bank][:, :].rearrange("p (t c) -> p t c", t=2),
                                               1.0 / (W_SCALE * W_SCALE), rows, ALU.mult, ALU.add).then_inc(side_free, 1)

            def context_low(n, g):
                dve.wait_ge(cx_high_ready, 2 * n + g + 1)
                nc.vector.tensor_tensor(cT[:, 1, g, :], tp_ps[:, :], cT[:, 0, g, :], ALU.subtract).then_inc(tp_free, 1)

            def unit(n, b, prev, nxt):
                for s in range(SLOTS):
                    now, split, late = (PROJECT_AT.get(s - i) for i in range(3))
                    if nxt:
                        for i in MAX_AT.get(s, ())[:1]:
                            maximum(n + 1, i)
                        if now is not None:
                            rope_products(n + 1, now)
                        if late is not None:
                            value_low(n + 1, 1 - b, late)
                        if split is not None:
                            high(n + 1, split)
                    if prev and s in CONTEXT_AT:
                        context_low(n - 1, CONTEXT_AT[s])
                    if prev and s in OUTPUT_AT:
                        residual(n - 1, 1 - b, OUTPUT_AT[s])
                    if not nxt and s - 1 in OUTPUT_AT and OUTPUT_AT[s - 1] % 2:
                        g = OUTPUT_AT[s - 1] // 2
                        dve.wait_ge(side_free, side_use(n, "output", OUTPUT_AT[s - 1])[0] + 1)
                        row_stats(nc, dve, g, s_stat, s_var, h, norm, NG)
                    if s - 1 in VALUES_AT and VALUES_AT[s - 1][1][-1] % 4 == 3:
                        normalize(n, VALUES_AT[s - 1][0], VALUES_AT[s - 1][1][-1] // 4)
                    if nxt:
                        for i in MAX_AT.get(s, ())[1:]:
                            maximum(n + 1, i)
                        if split is not None:
                            low(n + 1, split)
                        if s == max(MAX_AT):
                            negate(n + 1)
                normalize(n, 1, 1)

            dve.sem_inc(ctx_free, 1)
            for t in range(BT + 3):
                if t < BT:
                    rope_products(0, t)
                if 1 <= t <= BT:
                    value_low(0, 0, t - 1)
                    high(0, t - 1)
                    low(0, t - 1)
                for i in range(NMP):
                    if MPIECES[i][0] == t - 3:
                        maximum(0, i)
            negate(0)
            dve.wait_ge(wo_high_ready, 1)
            nc.vector.scalar_tensor_tensor(wo16[:, 1], wo_sb[:], W_SCALE, wo16[:, 0], ALU.mult,
                                           ALU.subtract).then_inc(wo_low_ready, 1)
            unit(0, 0, False, True)
            with dve.Fori(0, NP_ - 1) as p:
                unit(2 * p + 1, 1, True, True)
                unit(2 * p + 2, 0, True, True)
            unit(NU - 1, 1, True, False)
            for g in range(2):
                context_low(NU - 1, g)
                residual(NU - 1, 1, 2 * g)
                residual(NU - 1, 1, 2 * g + 1)


def experts(nc, sbt, sem, h, ident, norm, banks, router, weights, xs, ys, out, w_in, w_loaded):
    stats, mv, veps, std, rstd = norm
    ctx = ExitStack()
    with ctx:
        gates = sbt(ctx, "gates", [P, NT, 8], F32)
        tile_expert = sbt(ctx, "tile_expert", [1, SLOT_TILES], I32)
        gate_sb = sbt(ctx, "gate_sb", [P, 2, E, KC, FF], F16)
        up_sb = sbt(ctx, "up_sb", [P, 2, E, KC, FF], F16)
        down_sb = sbt(ctx, "down_sb", [P, 2, E, FC, DM], F16)
        pool_lo = sem(ctx, "pool_lo")
        dve_lo = sem(ctx, "dve_lo")
        tail_zero = sem(ctx, "tail_zero")
        with ExitStack() as c:
            route(nc, c, sbt, sem, h, ident, norm, banks, router, weights, xs, w_in, w_loaded,
                  gates, tile_expert, gate_sb, up_sb, down_sb, pool_lo, dve_lo, tail_zero)
        with ExitStack() as c:
            feed_forward(nc, c, sbt, sem, ident, banks, xs, ys, tile_expert, gate_sb, up_sb, down_sb,
                         pool_lo, dve_lo, tail_zero)
        with ExitStack() as c:
            combine(nc, c, sbt, sem, h, ys, gates, out)


def loads_before(m):
    return sum(16 * (2 if k % 3 == 2 else 1) for k in range(m % STAGES, m + 1, STAGES))


def matrix_parts(m, w_in, gate_sb, up_sb, down_sb):
    e, kind = m // 3, m % 3
    staged = w_in[:, m % STAGES, :]
    if kind < 2:
        w = (gate_sb, up_sb)[kind]
        return [(staged[:, 0:KC * FF], *(w[:, a, e].rearrange("p k f -> p (k f)") for a in range(2)))]
    full = FF // P
    return [(staged[:, 0:full * DM], *(down_sb[:, a, e, 0:full].rearrange("p c d -> p (c d)") for a in range(2))),
            (staged[0:FF % P, full * DM:], *(down_sb[0:FF % P, a, e, full] for a in range(2)))]


def route(nc, ctx, sbt, sem, h, ident, norm, banks, router, weights, xs, w_in, w_loaded,
          gates, tile_expert, gate_sb, up_sb, down_sb, pool_lo, dve_lo, tail_zero):
    stats, mv, veps, std, rstd = norm

    def sb(name, shape, dt):
        return sbt(ctx, name, shape, dt)

    def sm(name):
        return sem(ctx, name)

    xn = sb("xn2", [P, NT, ROW], F32)
    pos = sb("pos", [P, TOPK, NT], I32)
    xT = sb("xT2", [P, XB, 2 * KC, P], F32)
    router_sb = sb("router_sb", [P, KC, E], F32)
    logits = sb("logits", [P, NT, E], F32)
    shifted = sb("shifted", [P, NT, E], F32)
    expd = sb("expd", [P, NT, E], F32)
    rmax = sb("rmax", [P, NT], F32)
    total = sb("total", [P, NT], F32)
    inv = sb("inv", [P, NT], F32)
    pr = sb("pr", [P, NT, E], F32)
    idx = sb("idx", [P, NT, 8], U32)
    idxf = sb("idxf", [P, NT, 2], F32)
    iota_e = sb("iota_e", [P, E], F32)
    iota_t = sb("iota_t", [1, SLOT_TILES], F32)
    before = sb("before", [P, P], F32)
    ones = sb("ones", [P, P], F32)
    hot = sb("hot", [P, TOPK, NT, E], F32)
    chosen = sb("chosen", [P, NT, E], F32)
    cum = sb("cum", [P, 2, NT, E], F32)
    rank = sb("rank", [P, NT, E], F32)
    cnt_i = sb("cnt_i", [P, E], I32)
    cnt_s = sb("cnt_s", [P, E], I32)
    tiles = sb("tiles", [P, E], F32)
    ecum = sb("ecum", [P, 2, E], F32)
    base = sb("base", [P, E], F32)
    picked = sb("picked", [P, TOPK, NT, E], F32)
    posf = sb("posf", [P, TOPK, NT], F32)
    past = sb("past", [1, SLOT_TILES, E], F32)
    texp = sb("texp", [1, SLOT_TILES], F32)

    c_made, c_sel = sm("c_made"), sm("c_sel")
    r_in = sm("r_in")
    split_hi = sm("split_hi")
    stat, var, root, inv_root = sm("stat"), sm("var"), sm("root"), sm("inv_root")
    xn_ready, xtp, xt_ready, lg_ready = sm("xn_ready2"), sm("xtp2"), sm("xt_ready2"), sm("lg_ready2")
    sh_ready, ex_ready = sm("sh_ready"), sm("ex_ready")
    chosen_ready, ranks_ready, step_done, pos_ready = sm("chosen_ready"), sm("ranks_ready"), sm("step_done"), sm("pos_ready")
    scattered = [sm(f"scattered{g}") for g in range(NG)]
    index_ready = sm("index_ready")

    xt_banks = [banks[0], banks[1], banks[5]]

    block = ctx.enter_context(nc.Block())

    @block.sync
    def _(sp):
        sp.dma_start(router_sb[:, :, :].rearrange("p k e -> p (k e)"), router).then_inc(r_in, 16)
        for m in range(STAGES, MATRICES):
            if m - STAGES in POOL_MATRICES:
                sp.wait_ge(pool_lo, POOL_MATRICES.index(m - STAGES) + 1)
            else:
                sp.wait_ge(dve_lo, DVE_MATRICES.index(m - STAGES) + 1)
            load_matrix(sp, m, w_in, w_loaded, weights)

    @block.gpsimd
    def _(pool):
        nc.gpsimd.memset(down_sb[FF % P:P, :, :, FC - 1, :], 0.0).then_inc(tail_zero, 1)
        pool.wait_ge(tail_zero, 1)
        nc.gpsimd.iota(iota_e[:], pattern=[[1, E]], base=0, channel_multiplier=0,
                       allow_small_or_imprecise_dtypes=True).then_inc(c_made, 1)
        nc.gpsimd.iota(iota_t[:], pattern=[[1, SLOT_TILES]], base=0, channel_multiplier=0,
                       allow_small_or_imprecise_dtypes=True).then_inc(c_made, 1)
        nc.gpsimd.memset(ones[:], 1.0).then_inc(c_sel, 1)
        pool.wait_ge(c_sel, 1)
        nc.gpsimd.affine_select(out=before[:], in_=ones[:], compare_op=ALU.is_gt, fill=0.0, base=0,
                                pattern=[[1, P]], channel_multiplier=-1).then_inc(c_made, 1)
        nc.gpsimd.iota(xn[:, :, DM:ROW].bitcast(I32), pattern=[[P, NT], [1, 1]], base=0,
                       channel_multiplier=1).then_inc(index_ready, 1)
        for m in POOL_MATRICES:
            pool.wait_ge(split_hi, m + 1)
            for w32, hi, lo in matrix_parts(m, w_in, gate_sb, up_sb, down_sb):
                last = nc.gpsimd.tensor_tensor(lo, w32, hi, ALU.subtract)
            last.then_inc(pool_lo, 1)
        pool.wait_ge(pos_ready, 1)
        pool.wait_ge(index_ready, 1)
        for k in range(TOPK):
            for g in range(NG):
                if k > 0:
                    pool.wait_ge(scattered[g], 16 * GT * k)
                    nc.gpsimd.iota(xn[:, g * GT:(g + 1) * GT, DM:ROW].bitcast(I32), pattern=[[P, GT], [1, 1]],
                                   base=T * k + g * GT * P, channel_multiplier=1).then_inc(index_ready, 1)
                    pool.wait_ge(index_ready, NG * (k - 1) + g + 2)
                for t in range(g * GT, (g + 1) * GT):
                    nc.gpsimd.indirect_dma_start(
                        out=xs, out_offset=bass.IndirectOffsetOnAxis(ap=pos[:, k, t:t + 1], axis=0),
                        in_=xn[:, t, :], in_offset=None).then_inc(scattered[g], 16)
        for g in range(NG):
            pool.wait_ge(scattered[g], 16 * TOPK * GT)

    @block.scalar
    def _(act):
        def highs(m):
            act.wait_ge(w_loaded[m % STAGES], loads_before(m))
            for w32, hi, lo in matrix_parts(m, w_in, gate_sb, up_sb, down_sb):
                last = nc.scalar.activation(hi, w32, ACT.Copy, scale=W_SCALE)
                if m in POOL_MATRICES:
                    last = nc.scalar.activation(w32, w32, ACT.Copy, scale=W_SCALE)
            last.then_inc(split_hi, 1)

        def pair(i):
            act.wait_ge(xtp, i + 1)
            nc.scalar.activation(xT[:, i % XB].rearrange("p k t -> p (k t)"), xt_banks[i % XB][:, :],
                                 ACT.Copy).then_inc(xt_ready, 1)

        for g in range(NG // 2):
            row_roots(nc, act, g, None, root, norm)
        for m in range(HIGHS_UNTIL[0]):
            highs(m)
        for g in range(NG):
            if g < NG // 2:
                row_roots(nc, act, g + NG // 2, var, root, norm, -NG // 2)
            pair(2 * g)
            pair(2 * g + 1)
            for m in range(HIGHS_UNTIL[g], HIGHS_UNTIL[g + 1]):
                highs(m)
        act.wait_ge(sh_ready, 1)
        nc.scalar.activation(expd[:], shifted[:], ACT.Exp).then_inc(ex_ready, 1)
        for m in range(HIGHS_UNTIL[-1], MATRICES):
            highs(m)

    @block.tensor
    def _(pe):
        pe.wait_ge(r_in, 16)

        def logit(i):
            pe.wait_ge(xt_ready, i + 1)
            for t in (2 * i, 2 * i + 1):
                for kc in range(KC):
                    mm = nc.tensor.matmul(banks[2][:, t * E:(t + 1) * E], xT[:, i % XB, (t % 2) * KC + kc, :],
                                          router_sb[:, kc, :], start=(kc == 0), stop=(kc == KC - 1))
            mm.then_inc(lg_ready, 1)

        for i in range(NT // 2):
            pe.wait_ge(xn_ready, 2 * i + 2)
            if i >= XB:
                pe.wait_ge(xt_ready, i - XB + 1)
            for k in range(2 * KC):
                mm = nc.tensor.transpose(xt_banks[i % XB][:, k * P:(k + 1) * P],
                                         xn[:, 2 * i + k // KC, (k % KC) * P:(k % KC + 1) * P], ident[:])
            mm.then_inc(xtp, 1)
            if i >= 1:
                logit(i - 1)
        logit(NT // 2 - 1)
        pe.wait_ge(chosen_ready, 1)
        pe.wait_ge(c_made, 3)
        flat = chosen[:, :, :].rearrange("p t e -> p (t e)")
        nc.tensor.matmul(banks[3][:, 0:NT * E], before[:], flat, start=True, stop=True)
        nc.tensor.matmul(banks[4][:, 0:NT * E], ones[:], flat, start=True, stop=True).then_inc(ranks_ready, 1)

    @block.vector
    def _(dve):
        done = [0]

        def step(ins):
            done[0] += 1
            ins.then_inc(step_done, 1)
            dve.wait_ge(step_done, done[0])

        for g in range(NG):
            if g + NG // 2 < NG:
                row_stats(nc, dve, g + NG // 2, stat, var, h, norm, -NG // 2)
            normal_rows(nc, dve, g, root, inv_root, xn_ready, lambda t: xn[:, t, 0:DM], h, norm)

        def lows(m):
            dve.wait_ge(split_hi, m + 1)
            for w32, hi, lo in matrix_parts(m, w_in, gate_sb, up_sb, down_sb):
                last = nc.vector.scalar_tensor_tensor(lo, w32, W_SCALE, hi, ALU.mult, ALU.subtract)
            last.then_inc(dve_lo, 1)

        for m in DVE_MATRICES[:DVE_EARLY]:
            lows(m)
        dve.wait_ge(lg_ready, NT // 2)
        step(nc.vector.tensor_copy(logits[:, :, :].rearrange("p t e -> p (t e)"), banks[2][:, 0:NT * E]))
        step(nc.vector.reduce_max(rmax[:], logits[:], AX.X))
        nc.vector.tensor_tensor(shifted[:], logits[:], rmax[:, :].unsqueeze(2).to_broadcast([P, NT, E]),
                                ALU.subtract).then_inc(sh_ready, 1)
        dve.wait_ge(ex_ready, 1)
        step(nc.vector.reduce_sum(total[:], expd[:], AX.X))
        step(nc.vector.reciprocal(inv[:], total[:]))
        step(nc.vector.tensor_tensor(pr[:], expd[:], inv[:, :].unsqueeze(2).to_broadcast([P, NT, E]), ALU.mult))
        for t in range(NT):
            last = nc.vector.max(gates[:, t, :], pr[:, t, :])
        step(last)
        for t in range(NT):
            last = nc.vector.max_index(idx[:, t, :], gates[:, t, :], pr[:, t, :])
        step(last)
        step(nc.vector.tensor_copy(idxf[:], idx[:, :, 0:2]))
        dve.wait_ge(c_made, 3)
        for k in range(TOPK):
            last = nc.vector.tensor_tensor(hot[:, k], iota_e[:, :].unsqueeze(1).to_broadcast([P, NT, E]),
                                           idxf[:, :, k].unsqueeze(2).to_broadcast([P, NT, E]), ALU.is_equal)
        step(last)
        nc.vector.tensor_tensor(chosen[:], hot[:, 0], hot[:, 1], ALU.add).then_inc(chosen_ready, 1)
        dve.wait_ge(ranks_ready, 1)
        tile_cnt = banks[4][:, 0:NT * E].rearrange("p (t e) -> p t e", e=E)
        step(nc.vector.tensor_copy(cum[:, 0], tile_cnt))
        a, d = 0, 1
        while d < NT:
            nc.vector.tensor_copy(cum[:, 1 - a, 0:d, :], cum[:, a, 0:d, :])
            step(nc.vector.tensor_tensor(cum[:, 1 - a, d:NT, :], cum[:, a, d:NT, :], cum[:, a, 0:NT - d, :], ALU.add))
            a, d = 1 - a, 2 * d
        step(nc.vector.tensor_scalar(cnt_i[:], cum[:, a, NT - 1, :], float(P - 1), None, ALU.add))
        step(nc.vector.tensor_scalar(cnt_s[:], cnt_i[:], 7, None, ALU.arith_shift_right))
        step(nc.vector.tensor_copy(tiles[:], cnt_s[:]))
        step(nc.vector.tensor_copy(ecum[:, 0], tiles[:]))
        ea, d = 0, 1
        while d < E:
            nc.vector.tensor_copy(ecum[:, 1 - ea, 0:d], ecum[:, ea, 0:d])
            step(nc.vector.tensor_tensor(ecum[:, 1 - ea, d:E], ecum[:, ea, d:E], ecum[:, ea, 0:E - d], ALU.add))
            ea, d = 1 - ea, 2 * d
        step(nc.vector.tensor_tensor(base[:], ecum[:, ea], tiles[:], ALU.subtract))
        step(nc.vector.tensor_tensor(rank[:], cum[:, a], tile_cnt, ALU.subtract))
        step(nc.vector.tensor_tensor(rank[:], banks[3][:, 0:NT * E].rearrange("p (t e) -> p t e", e=E), rank[:], ALU.add))
        step(nc.vector.tensor_scalar(base[:], base[:], float(P), None, ALU.mult))
        step(nc.vector.tensor_tensor(rank[:], rank[:], base[:, :].unsqueeze(1).to_broadcast([P, NT, E]), ALU.add))
        for k in range(TOPK):
            last = nc.vector.tensor_tensor(picked[:, k], hot[:, k], rank[:], ALU.mult)
        step(last)
        step(nc.vector.reduce_sum(posf[:], picked[:], AX.X))
        nc.vector.tensor_copy(pos[:], posf[:]).then_inc(pos_ready, 1)
        step(nc.vector.tensor_tensor(past[:], iota_t[:, :].unsqueeze(2).to_broadcast([1, SLOT_TILES, E]),
                                     ecum[0:1, ea].unsqueeze(1).to_broadcast([1, SLOT_TILES, E]), ALU.is_ge))
        step(nc.vector.reduce_sum(texp[:], past[:], AX.X))
        step(nc.vector.tensor_scalar(tile_expert[:], texp[:], float(E - 1), None, ALU.min))
        for m in DVE_MATRICES[DVE_EARLY:]:
            lows(m)


def feed_forward(nc, ctx, sbt, sem, ident, banks, xs, ys, tile_expert, gate_sb, up_sb, down_sb,
                 pool_lo, dve_lo, tail_zero):
    def sb(name, shape, dt):
        return sbt(ctx, name, shape, dt)

    def sm(name):
        return sem(ctx, name)

    x_in = sb("x_in", [P, 2, ROW], F32)
    slot_of = sb("slot_index", [P, 2], I32)
    store_at = sb("store_index", [P, 2], I32)
    xT = sb("xT3", [P, 2, 2, KC, P], F16)
    sg = sb("sg", [P, FF], F32)
    hh = sb("hh", [P, FC * P], F32)
    hT = sb("hT", [P, 2, FC * P], F16)
    y_sb = sb("y_sb", [P, 2, DM], F32)

    x_loaded = [sm("x_loaded0"), sm("x_loaded1")]
    y_stored = [sm("y_stored0"), sm("y_stored1")]
    pad_zero, xt_tp, x_hi, x_lo = sm("pad_zero"), sm("xt_tp"), sm("x_hi"), sm("x_lo")
    index_in, index_kept, store_turn = sm("index_in"), sm("index_kept"), sm("store_turn")
    g_ready, u_ready, sg_ready, hh_ready = sm("g_ready"), sm("u_ready"), sm("sg_ready"), sm("hh_ready")
    ht_tp, ht_hi, ht_lo, y_ready, y_free = sm("ht_tp"), sm("ht_hi"), sm("ht_lo"), sm("y_ready3"), sm("y_free3")

    xt_ps = banks[0]
    y_ps = banks[1]
    ht_ps = banks[2:4]
    g_ps = banks[4:6]
    u_ps = banks[6:8]
    LAST = SLOT_TILES - 1
    assert LAST % 2 == 0
    ht_cols = [(0, 4 * P), (4 * P, FC * P)]

    def tiles(engine, step):
        with engine.Fori(0, LAST // 2 - 1) as i:
            for b in range(2):
                step(2 * i + 1 + b, 1 - b, True)
        step(LAST - 1, 1, True)
        step(LAST, 0, False)

    block = ctx.enter_context(nc.Block())

    @block.sync
    def _(sp):
        def load(j, b):
            sp.dma_start(x_in[:, b, :], xs[bass.ds(j * P, P), :]).then_inc(x_loaded[b], 16)

        def step(j, b):
            sp.wait_ge(index_in, j + 1)
            load(j + 2, b)

        load(0, 0)
        load(1, 1)
        with sp.Fori(0, LAST // 2 - 1) as i:
            for b in range(2):
                step(2 * i + b, b)
        step(LAST - 2, 0)

    @block.gpsimd
    def _(pool):
        def store(j, b, earlier):
            pool.wait_ge(y_free, j + 2)
            if not (isinstance(earlier, int) and earlier == 0):
                pool.wait_ge(y_stored[1 - b], 16 * earlier)
            pool.sem_inc(store_turn, 1)
            nc.gpsimd.indirect_dma_start(
                out=ys, out_offset=bass.IndirectOffsetOnAxis(ap=store_at[:, b:b + 1], axis=0),
                in_=y_sb[:, b, :], in_offset=None).then_inc(y_stored[b], 16)

        store(0, 0, 0)
        store(1, 1, 1)
        with pool.Fori(1, LAST // 2) as i:
            for b in range(2):
                store(2 * i + b, b, i + b)
        store(LAST, 0, LAST // 2)
        pool.wait_ge(y_stored[0], 16 * (LAST // 2 + 1))
        pool.wait_ge(y_stored[1], 16 * (LAST // 2))

    @block.scalar
    def _(act):
        def x_high(j, b):
            act.wait_ge(xt_tp, j + 1)
            nc.scalar.activation(xT[:, b, 0].rearrange("p k t -> p (k t)"), xt_ps[:, 0:KC * P],
                                 ACT.Copy).then_inc(x_hi, 1)

        def silu(j):
            act.wait_ge(g_ready, j + 1)
            for c in range(2):
                last = nc.scalar.activation(sg[:, c * FH:(c + 1) * FH], g_ps[c][:, 0:FH], ACT.Silu,
                                            scale=1.0 / W_SCALE)
            last.then_inc(sg_ready, 1)

        def hidden_high(j):
            act.wait_ge(ht_tp, j + 1)
            for c, (lo, hi) in enumerate(ht_cols):
                nc.scalar.activation(hT[:, 0, lo:hi], ht_ps[c][:, 0:hi - lo], ACT.Copy).then_inc(ht_hi, 1)

        def step(j, b, more):
            hidden_high(j - 1)
            if more:
                x_high(j + 1, 1 - b)
            silu(j)

        x_high(0, 0)
        x_high(1, 1)
        silu(0)
        tiles(act, step)
        hidden_high(LAST)

    @block.vector
    def _(dve):
        def x_low(j, b):
            dve.wait_ge(x_hi, j + 1)
            nc.vector.tensor_tensor(xT[:, b, 1].rearrange("p k t -> p (k t)"), xt_ps[:, 0:KC * P],
                                    xT[:, b, 0].rearrange("p k t -> p (k t)"), ALU.subtract).then_inc(x_lo, 1)
            if not (isinstance(j, int) and j < 2):
                dve.wait_ge(index_kept, j - 1)
            nc.vector.tensor_copy(slot_of[:, b:b + 1], x_in[:, b, DM:ROW].bitcast(I32)).then_inc(index_in, 1)

        def keep_index(j, b, stored):
            dve.wait_ge(index_in, j + 1)
            if not (isinstance(stored, int) and stored == 0):
                dve.wait_ge(y_stored[b], 16 * stored)
            nc.vector.tensor_copy(store_at[:, b:b + 1], slot_of[:, b:b + 1]).then_inc(index_kept, 1)

        def gated(j):
            dve.wait_ge(sg_ready, j + 1)
            dve.wait_ge(u_ready, j + 1)
            for c in range(2):
                last = nc.vector.scalar_tensor_tensor(hh[:, c * FH:(c + 1) * FH], u_ps[c][:, 0:FH], 1.0 / W_SCALE,
                                                      sg[:, c * FH:(c + 1) * FH], ALU.mult, ALU.mult)
            last.then_inc(hh_ready, 1)

        def hidden_low(j):
            for c, (lo, hi) in enumerate(ht_cols):
                dve.wait_ge(ht_hi, 2 * j + c + 1)
                last = nc.vector.tensor_tensor(hT[:, 1, lo:hi], ht_ps[c][:, 0:hi - lo], hT[:, 0, lo:hi], ALU.subtract)
            last.then_inc(ht_lo, 1)

        def y_copy(j, b):
            dve.wait_ge(y_ready, j + 1)
            nc.vector.tensor_scalar(y_sb[:, b, :], y_ps[:, 0:DM], 1.0 / W_SCALE, None, ALU.mult).then_inc(y_free, 1)

        def step(j, b, stored, more):
            hidden_low(j - 1)
            keep_index(j - 1, 1 - b, stored)
            if more:
                x_low(j + 1, 1 - b)
            gated(j)
            y_copy(j - 1, 1 - b)

        nc.vector.memset(hh[:, FF:FC * P], 0.0).then_inc(pad_zero, 1)
        dve.sem_inc(y_free, 1)
        x_low(0, 0)
        x_low(1, 1)
        gated(0)
        step(1, 1, 0, True)
        step(2, 0, 0, True)
        with dve.Fori(1, LAST // 2 - 1) as i:
            for b in range(2):
                step(2 * i + 1 + b, 1 - b, i, True)
        step(LAST - 1, 1, LAST // 2 - 1, True)
        step(LAST, 0, LAST // 2 - 1, False)
        hidden_low(LAST)
        keep_index(LAST, 0, LAST // 2)
        y_copy(LAST, 0)

    @block.tensor
    def _(pe):
        pe.wait_ge(pool_lo, len(POOL_MATRICES))
        pe.wait_ge(dve_lo, len(DVE_MATRICES))
        pe.wait_ge(tail_zero, 1)
        pe.wait_ge(pad_zero, 1)

        def x_transpose(j, b, loads):
            pe.wait_ge(x_loaded[b], 16 * loads)
            if not (isinstance(j, int) and j == 0):
                pe.wait_ge(x_lo, j)
            for kc in range(KC):
                mm = nc.tensor.transpose(xt_ps[:, kc * P:(kc + 1) * P], x_in[:, b, kc * P:(kc + 1) * P], ident[:])
            mm.then_inc(xt_tp, 1)

        def gate_up(j, b):
            e = nc.tensor.value_load(tile_expert[0:1, bass.ds(j, 1)], min_val=0, max_val=E - 1)
            pe.wait_ge(x_lo, j + 1)
            for w, ps, ready in ((gate_sb, g_ps, g_ready), (up_sb, u_ps, u_ready)):
                for kc in range(KC):
                    for a, d in ((0, 0), (0, 1), (1, 0)):
                        for c in range(2):
                            mm = nc.tensor.matmul(ps[c][:, 0:FH], xT[:, b, a, kc, :],
                                                  w[:, d, bass.ds(e, 1), kc, c * FH:(c + 1) * FH].rearrange("p o f -> p (o f)"),
                                                  start=(kc == 0 and a == 0 and d == 0), stop=(kc == KC - 1 and a == 1))
                mm.then_inc(ready, 1)

        def hidden_transpose(j):
            pe.wait_ge(hh_ready, j + 1)
            for c in range(FC):
                mm = nc.tensor.transpose(ht_ps[c // 4][:, (c % 4) * P:(c % 4 + 1) * P], hh[:, c * P:(c + 1) * P], ident[:])
            mm.then_inc(ht_tp, 1)

        def down_proj(j):
            e = nc.tensor.value_load(tile_expert[0:1, bass.ds(j, 1)], min_val=0, max_val=E - 1)
            pe.wait_ge(ht_lo, j + 1)
            pe.wait_ge(y_free, j + 1)
            for c in range(FC):
                for a, d in ((0, 0), (0, 1), (1, 0)):
                    mm = nc.tensor.matmul(y_ps[:, 0:DM], hT[:, a, c * P:(c + 1) * P],
                                          down_sb[:, d, bass.ds(e, 1), c, :].rearrange("p o d -> p (o d)"),
                                          start=(c == 0 and a == 0 and d == 0), stop=(c == FC - 1 and a == 1))
            mm.then_inc(y_ready, 1)

        def step(j, b, loads, more):
            hidden_transpose(j - 1)
            if more:
                x_transpose(j + 1, 1 - b, loads)
            gate_up(j, b)
            down_proj(j - 1)

        x_transpose(0, 0, 1)
        x_transpose(1, 1, 1)
        gate_up(0, 0)
        with pe.Fori(0, LAST // 2 - 1) as i:
            for b in range(2):
                step(2 * i + 1 + b, 1 - b, i + 2, True)
        step(LAST - 1, 1, LAST // 2 + 1, True)
        step(LAST, 0, 0, False)
        hidden_transpose(LAST)
        down_proj(LAST)


def combine(nc, ctx, sbt, sem, h, ys, gates, out):
    ring = 3
    y = sbt(ctx, "y_choices", [P, ring, TOPK, GT, DM], F32)
    y_in = [sem(ctx, f"y_in{g}") for g in range(NG)]
    first_added, added, stored = sem(ctx, "first_added"), sem(ctx, "added"), sem(ctx, "stored")
    block = ctx.enter_context(nc.Block())

    @block.sync
    def _(sp):
        for g in range(NG):
            if g >= ring:
                sp.wait_ge(added, g - ring + 1)
            for k in range(TOPK):
                rows = ys[k * T + g * GT * P:k * T + (g + 1) * GT * P, :]
                sp.dma_start(y[:, g % ring, k],
                             rows.rearrange("(t p) d -> p t d", p=P)).then_inc(y_in[g], 16)

    @block.vector
    def _(dve):
        for g in range(NG):
            dve.wait_ge(y_in[g], 16 * TOPK)
            for k, done in enumerate((first_added, added)):
                if k > 0:
                    dve.wait_ge(first_added, g + 1)
                for t in range(GT * g, GT * (g + 1)):
                    last = nc.vector.scalar_tensor_tensor(h[:, t, :], y[:, g % ring, k, t % GT, :], gates[:, t, k:k + 1], h[:, t, :],
                                                          ALU.mult, ALU.add)
                last.then_inc(done, 1)

    @block.scalar
    def _(act):
        for g in range(NG):
            act.wait_ge(added, g + 1)
            act.dma_start(out[g * GT * P:(g + 1) * GT * P, :].rearrange("(t p) d -> p t d", p=P),
                          h[:, g * GT:(g + 1) * GT, :]).then_inc(stored, 16)
        act.wait_ge(stored, 16 * NG)


def rope_tables():
    half = D // 2
    fraction = (np.float32(2.0) * np.arange(half, dtype=np.float32) / np.float32(D)).astype(np.float32)
    timescale = (np.float32(10000.0) ** fraction).astype(np.float32)
    angle = (np.arange(S, dtype=np.float32)[:, None] / timescale).astype(np.float32)
    sin, cos = np.sin(angle), np.cos(angle)
    scale = np.array([D ** -0.5, D ** -0.5, 1.0, 1.0], np.float32) / np.float32(W_SCALE)

    def lay(a):
        a = (a[:, None, :] * scale[None, :, None]).astype(np.float32)
        return np.ascontiguousarray(a.reshape(BT, P, 4, D).transpose(1, 0, 2, 3)).reshape(P, BT * 4 * D)

    return lay(np.concatenate([cos, cos], 1)), lay(np.concatenate([-sin, sin], 1))


def kernel(x, L0_tok_W, L0_attn_wqkv, L0_attn_wo, L0_ffn_router_w, L0_ffn_gate_w, L0_ffn_up_w, L0_ffn_down_w):
    import concourse.bacc as _bacc
    from concourse.bass_utils import run_bass_kernel_spmd as _run

    rope_c, rope_s = rope_tables()
    wqkv = np.asarray(L0_attn_wqkv).reshape(KC, P, 3, NP_, 128).transpose(1, 0, 3, 2, 4)

    def up_layout(w):
        return np.asarray(w).transpose(0, 2, 1).reshape(E, KC, P, FF).transpose(0, 2, 1, 3).reshape(E, P, KC * FF)

    arrays = {
        "ids": np.asarray(x).reshape(NT, P).T,
        "emb": np.asarray(L0_tok_W),
        "wqkv": wqkv.reshape(P, KC * NP_ * 384),
        "wo": np.asarray(L0_attn_wo).reshape(NP_, P, DM).transpose(1, 0, 2).reshape(P, NP_ * DM),
        "router": np.asarray(L0_ffn_router_w).T.reshape(KC, P, E).transpose(1, 0, 2).reshape(P, KC * E),
        "gate": up_layout(L0_ffn_gate_w),
        "up": up_layout(L0_ffn_up_w),
        "down": np.asarray(L0_ffn_down_w).transpose(0, 2, 1),
        "rope_c": rope_c,
        "rope_s": rope_s,
    }
    arrays = {name: np.ascontiguousarray(a) for name, a in arrays.items()}
    nc = _bacc.Bacc("TRN2", target_bir_lowering=False, num_devices=1)
    args = [nc.dram_tensor(name, a.shape, mybir.dt.from_np(a.dtype), kind="ExternalInput").ap()
            for name, a in arrays.items()]
    out = nc.dram_tensor("out", (T, DM), F32, kind="ExternalOutput").ap()
    program(nc, *args, out)
    r = _run(nc, [arrays], core_ids=[0])
    return r.results[0]["out"].reshape(B, S, DM)
```
